# Optimizing a Trainium2 kernel written in Bass

```python
import numpy as np
import jax
import jax.numpy as jnp

def _softmax(x, axis=-1):
    return jax.nn.softmax(x, axis=axis)

def _gelu(x):
    return jax.nn.gelu(x, approximate=True)

def _silu(x):
    return jax.nn.silu(x)

def _sigmoid(x):
    return jax.nn.sigmoid(x)

def _layernorm(x, axis=-1, eps=1e-05):
    m = jnp.mean(x, axis=axis, keepdims=True)
    v = jnp.var(x, axis=axis, keepdims=True)
    return (x - m) / jnp.sqrt(v + eps)

def _scatter_add(tgt, idx, src, axis=0):
    return tgt.at[idx].add(src)

def _segment_sum(src, seg, n):
    return jax.ops.segment_sum(src, seg, n)
kernel_name = 'mk_flamingo_gated_d2_seqx_r8_1c8099'

def setup_inputs(seed: int=0):
    np.random.seed(seed)
    _w = jnp.asarray

    def _rec_inputs():
        import jax
        import jax.numpy as jnp
        _rk = jax.random.key(seed)
        x = -0.0002928 + 1 * jax.random.normal(jax.random.fold_in(_rk, 1), (8, 128, 128), jnp.float32)
        _lenS = 128 - jax.random.randint(jax.random.fold_in(_rk, 7), (8,), 0, max(1, 128 // 4) + 1, jnp.int32)
        _lenS2 = 128 - jax.random.randint(jax.random.fold_in(_rk, 8), (8,), 0, max(1, 128 // 4) + 1, jnp.int32)
        _ctx_1024P = jax.random.normal(jax.random.fold_in(_rk, 11), (8, 16, 128), jnp.float32)
        _ctx_1024c = jax.random.dirichlet(jax.random.fold_in(_rk, 511), 0.3 * jnp.ones((16,), jnp.float32), (8, 128))
        _ctx_1024t = jnp.einsum('bsk,bkd->bsd', _ctx_1024c, _ctx_1024P)
        _ctx_1024t = _ctx_1024t * jax.lax.rsqrt(jnp.mean(jnp.square(_ctx_1024t)) + 1e-12) * 0.953939
        ctx_1024 = -1.39393e-06 + 0.999914 * (_ctx_1024t + 0.3 * jax.random.normal(jax.random.fold_in(_rk, 611), (8, 128, 128), jnp.float32))
        _validS = jnp.arange(128)[None, :] < _lenS[:, None]
        _validS2 = jnp.arange(128)[None, :] < _lenS2[:, None]
        _causal = jnp.tril(jnp.ones((128, 128), dtype=bool))
        mask_BxS2_bf0 = jnp.logical_not(jnp.ones((8, 128), dtype=bool))
        _g = jax.random.normal(jax.random.fold_in(_rk, 9001), (2, 2), jnp.float32)
        _g = jnp.sign(_g) * jnp.maximum(jnp.abs(_g), 1.0) + (_g == 0) * 1.0
        g_xattn = _g[0]
        g_ffn = _g[1]
        return (x, ctx_1024, mask_BxS2_bf0, g_xattn, g_ffn)
    x, ctx_1024, mask_BxS2_bf0, g_xattn, g_ffn = _rec_inputs()

    def _L0_xattn_setup():
        import jax, jax.numpy as jnp
        import numpy as np
        DIM = 128
        HEADS = 16
        DIM_HEAD = 64
        INNER = HEADS * DIM_HEAD
        B, N = (2, 256)
        SCALE = DIM_HEAD ** (-0.5)
        key = jax.random.key(seed)
        ks = jax.random.split(key, 9)
        s_in = 1.0 / np.sqrt(DIM)
        s_inner = 1.0 / np.sqrt(INNER)
        return {'q': jax.random.normal(ks[0], (B, N, DIM), jnp.float32), 'k': jax.random.normal(ks[1], (B, N, DIM), jnp.float32), 'v': jax.random.normal(ks[2], (B, N, DIM), jnp.float32), 'Wq': jax.random.normal(ks[3], (DIM, INNER), jnp.float32) * s_in, 'Wk': jax.random.normal(ks[4], (DIM, INNER), jnp.float32) * s_in, 'Wv': jax.random.normal(ks[5], (DIM, INNER), jnp.float32) * s_in, 'Wo': jax.random.normal(ks[6], (INNER, DIM), jnp.float32) * s_inner, 'bo': jax.random.normal(ks[7], (DIM,), jnp.float32) * s_inner, 'mask': jnp.zeros((B, N), dtype=bool)}
    _L0_xattn_all = _L0_xattn_setup()
    _L0_xattn_in = {k: v for k, v in _L0_xattn_all.items() if k in ('Wq', 'Wk', 'Wv', 'Wo', 'bo')}
    del _L0_xattn_all

    def _L0_ffn_setup():
        import jax, jax.numpy as jnp
        import numpy as np
        B, S, D = (2, 256, 128)
        DFF = 256
        E_FFN = 8
        E_ZERO = 4
        E_TOT = E_FFN + E_ZERO
        TOP_K = 2
        key = jax.random.key(seed)
        k1, k2, k3, k4 = jax.random.split(key, 4)
        x = jax.random.normal(k1, (B, S, D), dtype=jnp.float32)
        gate_w = jax.random.normal(k2, (E_TOT, D), dtype=jnp.float32) * (1.0 / np.sqrt(D))
        expert_bias = jnp.zeros((E_TOT,), dtype=jnp.float32)
        w1 = jax.random.normal(k3, (E_FFN, DFF, D), dtype=jnp.float32) * (1.0 / np.sqrt(D))
        w2 = jax.random.normal(k4, (E_FFN, D, DFF), dtype=jnp.float32) * (1.0 / np.sqrt(DFF))
        return {'x': x, 'gate_w': gate_w, 'expert_bias': expert_bias, 'w1': w1, 'w2': w2}
    _L0_ffn_all = _L0_ffn_setup()
    _L0_ffn_in = {k: v for k, v in _L0_ffn_all.items() if k in ('gate_w', 'expert_bias', 'w1', 'w2')}
    del _L0_ffn_all

    def _L1_xattn_setup():
        import jax, jax.numpy as jnp
        import numpy as np
        D_MODEL = 128
        NUM_HEADS = 16
        D_HEAD = D_MODEL // NUM_HEADS
        B, LQ, LK = (4, 256, 256)
        key = jax.random.key(seed)
        ks = jax.random.split(key, 11)
        s = 1.0 / np.sqrt(D_MODEL)
        return {'query': jax.random.normal(ks[0], (B, LQ, D_MODEL), jnp.float32), 'key': jax.random.normal(ks[1], (B, LK, D_MODEL), jnp.float32), 'value': jax.random.normal(ks[2], (B, LK, D_MODEL), jnp.float32), 'Wq': jax.random.normal(ks[3], (D_MODEL, D_MODEL), jnp.float32) * s, 'bq': jax.random.normal(ks[4], (D_MODEL,), jnp.float32) * s, 'Wk': jax.random.normal(ks[5], (D_MODEL, D_MODEL), jnp.float32) * s, 'bk': jax.random.normal(ks[6], (D_MODEL,), jnp.float32) * s, 'Wv': jax.random.normal(ks[7], (D_MODEL, D_MODEL), jnp.float32) * s, 'bv': jax.random.normal(ks[8], (D_MODEL,), jnp.float32) * s, 'Wo': jax.random.normal(ks[9], (D_MODEL, D_MODEL), jnp.float32) * s, 'bo': jax.random.normal(ks[10], (D_MODEL,), jnp.float32) * s}
    _L1_xattn_all = _L1_xattn_setup()
    _L1_xattn_in = {k: v for k, v in _L1_xattn_all.items() if k in ('Wq', 'bq', 'Wk', 'bk', 'Wv', 'bv', 'Wo', 'bo')}
    del _L1_xattn_all

    def _L1_ffn_setup():
        import jax, jax.numpy as jnp
        import numpy as np
        BEST_K = 2

        def _expert(xf, w1, w3, w2):
            return jax.nn.silu(xf @ w1) * (xf @ w3) @ w2
        key = jax.random.key(seed)
        ks = jax.random.split(key, 9)
        E, S_sh, D, H = (8, 2, 128, 64)
        B, S = (2, 256)
        w = lambda k, shape: jax.random.normal(k, shape, dtype=jnp.float32) * 0.02
        return {'x': jax.random.normal(ks[0], (B, S, D), dtype=jnp.float32), 'router_w': w(ks[1], (D, E)), 'router_b': jnp.zeros((E,), dtype=jnp.float32), 'routed_w1': w(ks[2], (E, D, H)), 'routed_w3': w(ks[3], (E, D, H)), 'routed_w2': w(ks[4], (E, H, D)), 'shared_w1': w(ks[5], (S_sh, D, H)), 'shared_w3': w(ks[6], (S_sh, D, H)), 'shared_w2': w(ks[7], (S_sh, H, D))}
    _L1_ffn_all = _L1_ffn_setup()
    _L1_ffn_in = {k: v for k, v in _L1_ffn_all.items() if k in ('router_w', 'router_b', 'routed_w1', 'routed_w3', 'routed_w2', 'shared_w1', 'shared_w3', 'shared_w2')}
    del _L1_ffn_all
    return {'x': x, 'ctx_1024': ctx_1024, 'mask_BxS2_bf0': mask_BxS2_bf0, 'g_xattn': g_xattn, 'g_ffn': g_ffn, 'L0_xattn_Wq': _L0_xattn_in['Wq'], 'L0_xattn_Wk': _L0_xattn_in['Wk'], 'L0_xattn_Wv': _L0_xattn_in['Wv'], 'L0_xattn_Wo': _L0_xattn_in['Wo'], 'L0_xattn_bo': _L0_xattn_in['bo'], 'L0_ffn_gate_w': _L0_ffn_in['gate_w'], 'L0_ffn_expert_bias': _L0_ffn_in['expert_bias'], 'L0_ffn_w1': _L0_ffn_in['w1'], 'L0_ffn_w2': _L0_ffn_in['w2'], 'L1_xattn_Wq': _L1_xattn_in['Wq'], 'L1_xattn_bq': _L1_xattn_in['bq'], 'L1_xattn_Wk': _L1_xattn_in['Wk'], 'L1_xattn_bk': _L1_xattn_in['bk'], 'L1_xattn_Wv': _L1_xattn_in['Wv'], 'L1_xattn_bv': _L1_xattn_in['bv'], 'L1_xattn_Wo': _L1_xattn_in['Wo'], 'L1_xattn_bo': _L1_xattn_in['bo'], 'L1_ffn_router_w': _L1_ffn_in['router_w'], 'L1_ffn_router_b': _L1_ffn_in['router_b'], 'L1_ffn_routed_w1': _L1_ffn_in['routed_w1'], 'L1_ffn_routed_w3': _L1_ffn_in['routed_w3'], 'L1_ffn_routed_w2': _L1_ffn_in['routed_w2'], 'L1_ffn_shared_w1': _L1_ffn_in['shared_w1'], 'L1_ffn_shared_w3': _L1_ffn_in['shared_w3'], 'L1_ffn_shared_w2': _L1_ffn_in['shared_w2']}

def reference(x, ctx_1024, mask_BxS2_bf0, g_xattn, g_ffn, L0_xattn_Wq, L0_xattn_Wk, L0_xattn_Wv, L0_xattn_Wo, L0_xattn_bo, L0_ffn_gate_w, L0_ffn_expert_bias, L0_ffn_w1, L0_ffn_w2, L1_xattn_Wq, L1_xattn_bq, L1_xattn_Wk, L1_xattn_bk, L1_xattn_Wv, L1_xattn_bv, L1_xattn_Wo, L1_xattn_bo, L1_ffn_router_w, L1_ffn_router_b, L1_ffn_routed_w1, L1_ffn_routed_w3, L1_ffn_routed_w2, L1_ffn_shared_w1, L1_ffn_shared_w3, L1_ffn_shared_w2):
    import jax
    import jax.numpy as jnp

    def _L0_xattn_ref(q, k, v, Wq, Wk, Wv, Wo, bo, mask):
        import jax, jax.numpy as jnp
        import numpy as np
        DIM = 128
        HEADS = 16
        DIM_HEAD = 64
        INNER = HEADS * DIM_HEAD
        B, N = (2, 256)
        SCALE = DIM_HEAD ** (-0.5)
        b, n, _ = q.shape
        h, d = (HEADS, DIM_HEAD)

        def split_heads(x):
            return x.reshape(b, n, h, d).transpose(0, 2, 1, 3)
        qh = split_heads(q @ Wq)
        kh = split_heads(k @ Wk)
        vh = split_heads(v @ Wv)
        dots = jnp.einsum('bhid,bhjd->bhij', qh, kh) * SCALE
        mask_value = -jnp.finfo(dots.dtype).max
        dots = jnp.where(mask[:, None, None, :], mask_value, dots)
        causal = jnp.triu(jnp.ones((n, n), dtype=bool), k=1)
        dots = jnp.where(causal[None, None, :, :], mask_value, dots)
        attn = jax.nn.softmax(dots, axis=-1)
        out = jnp.einsum('bhij,bhjd->bhid', attn, vh)
        out = out.transpose(0, 2, 1, 3).reshape(b, n, h * d)
        return out @ Wo + bo

    def _L0_ffn_ref(x, gate_w, expert_bias, w1, w2):
        import jax, jax.numpy as jnp
        import numpy as np
        B, S, D = (2, 256, 128)
        DFF = 256
        E_FFN = 8
        E_ZERO = 4
        E_TOT = E_FFN + E_ZERO
        TOP_K = 2
        logits = jnp.einsum('btd,ed->bte', x, gate_w) + expert_bias
        topk_logits, topk_idx = jax.lax.top_k(logits, TOP_K)
        topk_w = jax.nn.softmax(topk_logits, axis=-1)
        onehot = jax.nn.one_hot(topk_idx, E_TOT, dtype=x.dtype)
        w = jnp.einsum('btk,btke->bte', topk_w, onehot)
        w_ffn = w[..., :E_FFN]
        w_zero = jnp.sum(w[..., E_FFN:], axis=-1)
        h = jax.nn.silu(jnp.einsum('btd,efd->btef', x, w1))
        y = jnp.einsum('btef,edf->bted', h, w2)
        out = jnp.einsum('bte,bted->btd', w_ffn, y) + w_zero[..., None] * x
        return out

    def _L1_xattn_ref(query, key, value, Wq, bq, Wk, bk, Wv, bv, Wo, bo):
        import jax, jax.numpy as jnp
        import numpy as np
        D_MODEL = 128
        NUM_HEADS = 16
        D_HEAD = D_MODEL // NUM_HEADS
        B, LQ, LK = (4, 256, 256)
        b = query.shape[0]
        q = (query @ Wq.T + bq).reshape(b, -1, NUM_HEADS, D_HEAD)
        k = (key @ Wk.T + bk).reshape(b, -1, NUM_HEADS, D_HEAD)
        v = (value @ Wv.T + bv).reshape(b, -1, NUM_HEADS, D_HEAD)
        scale = 1.0 / np.sqrt(D_HEAD).astype(np.float32)
        attn = jnp.einsum('bqhd,bkhd->bhqk', q, k) * scale
        attn = jax.nn.softmax(attn, axis=-1)
        out = jnp.einsum('bhqk,bkhd->bqhd', attn, v).reshape(b, -1, D_MODEL)
        return out @ Wo.T + bo

    def _L1_ffn_ref(x, router_w, router_b, routed_w1, routed_w3, routed_w2, shared_w1, shared_w3, shared_w2):
        import jax, jax.numpy as jnp
        import numpy as np
        BEST_K = 2

        def _expert(xf, w1, w3, w2):
            return jax.nn.silu(xf @ w1) * (xf @ w3) @ w2
        B, S, D = x.shape
        T = B * S
        xf = x.reshape(T, D)
        logits = xf @ router_w + router_b
        topk_vals, topk_idx = jax.lax.top_k(logits, BEST_K)
        sparse = jnp.full_like(logits, -jnp.inf)
        sparse = sparse.at[jnp.arange(T)[:, None], topk_idx].set(topk_vals)
        gates = jax.nn.softmax(sparse, axis=-1)
        routed = jax.vmap(_expert, in_axes=(None, 0, 0, 0))(xf, routed_w1, routed_w3, routed_w2)
        routed_out = jnp.einsum('etd,te->td', routed, gates)
        shared_out = jax.vmap(_expert, in_axes=(None, 0, 0, 0))(xf, shared_w1, shared_w3, shared_w2).sum(axis=0)
        return (routed_out + shared_out).reshape(B, S, D)
    x = x + jnp.tanh(g_xattn[0]) * _L0_xattn_ref(_layernorm(x, axis=-1), ctx_1024, ctx_1024, L0_xattn_Wq, L0_xattn_Wk, L0_xattn_Wv, L0_xattn_Wo, L0_xattn_bo, mask_BxS2_bf0)
    x = x + jnp.tanh(g_ffn[0]) * _L0_ffn_ref(_layernorm(x, axis=-1), L0_ffn_gate_w, L0_ffn_expert_bias, L0_ffn_w1, L0_ffn_w2)
    x = x + jnp.tanh(g_xattn[1]) * _L1_xattn_ref(_layernorm(x, axis=-1), ctx_1024, ctx_1024, L1_xattn_Wq, L1_xattn_bq, L1_xattn_Wk, L1_xattn_bk, L1_xattn_Wv, L1_xattn_bv, L1_xattn_Wo, L1_xattn_bo)
    x = x + jnp.tanh(g_ffn[1]) * _L1_ffn_ref(_layernorm(x, axis=-1), L1_ffn_router_w, L1_ffn_router_b, L1_ffn_routed_w1, L1_ffn_routed_w3, L1_ffn_routed_w2, L1_ffn_shared_w1, L1_ffn_shared_w3, L1_ffn_shared_w2)
    return x

_drawn_inputs = setup_inputs


def setup_inputs(seed=0):
    import zlib

    import numpy as np

    out = dict(_drawn_inputs(seed))
    spreads = {'g_ffn': (-1.0, 0.6), 'L0_ffn_expert_bias': (0.0, 0.1), 'L1_ffn_router_b': (0.0, 0.8)}
    factors = {'L1_xattn_bq': 2.918,
     'L1_xattn_bk': 8.0,
     'L1_ffn_router_w': 8.0,
     'L1_ffn_routed_w1': 8.0,
     'L1_ffn_routed_w3': 8.0,
     'L1_ffn_routed_w2': 8.0,
     'L1_ffn_shared_w1': 8.0,
     'L1_ffn_shared_w3': 8.0,
     'L1_ffn_shared_w2': 8.0}
    for name, (base, spread) in spreads.items():
        noise = np.random.default_rng([zlib.crc32(name.encode()), seed]).standard_normal(out[name].shape)
        drawn = base * np.exp(spread * noise) if base else spread * noise
        out[name] = jnp.asarray(drawn.astype(out[name].dtype))
    for name, factor in factors.items():
        out[name] = (out[name] * factor).astype(out[name].dtype)
    return out
```

```python
from contextlib import ExitStack

import concourse.bass as bass
from concourse import mybir

F32 = mybir.dt.float32
F32R = mybir.dt.float32r
BF16 = mybir.dt.bfloat16
U8 = mybir.dt.uint8
ALU = mybir.AluOpType
ACT = mybir.ActivationFunctionType
X = mybir.AxisListType.X

P = 128
B = 8
T = B * P
HALF = T // 2
HB = B // 2
H4 = 4
G = 4
DH0 = 64
SCALE0 = DH0 ** -0.5
DH1 = 8
SCALE1 = DH1 ** -0.5
GR = H4 * DH1
E0, E0F, F0 = 12, 8, 256
E1, E1S = 8, 10
F1 = 64
C0 = F0 // P
C1 = E1S * F1 // P
MASKED = -float(2 ** 100)
EPS = 1e-5
BANKS = 12


def build(nc, x, ctxT, mask, g_x, g_f, w0, wo0, bo0, gw0, gb0, f0w1, f0w2,
          wqk1, bqk1, wv1, bv1, wo1, bo1, gw1, gb1, f1w13, f1w2,
          ident, causal, lo_row, head_row, rev0, rev1, out):
    with ExitStack() as ctx:
        def sb(name, shape, dt=F32):
            return ctx.enter_context(nc.sbuf_tensor(name, shape, dt))

        def sem(name):
            return ctx.enter_context(nc.semaphore(name))

        x_sb = sb("x_sb", [P, B, P])
        ctx_f = sb("ctx_f", [P, T])
        mask_u8 = sb("mask_u8", [P, T], U8)
        gates_in = sb("gates_in", [P, 4])
        col = sb("col", [P, 8])
        bscale = sb("bscale", [P, 2])
        bqk = sb("bqk", [P, 2])
        gw0_sb = sb("gw0_sb", [P, E0])
        gw1_sb = sb("gw1_sb", [P, E1])
        gb0_sb = sb("gb0_sb", [P, E0])
        gb1_sb = sb("gb1_sb", [P, E1])
        rev0_sb = sb("rev0_sb", [P, E0])
        rev1_sb = sb("rev1_sb", [P, E1])
        wv1_sb = sb("wv1_sb", [P, P])
        bv1_sb = sb("bv1_sb", [P, P])
        id_sb = sb("id_sb", [P, P])
        causal_sb = sb("causal_sb", [P, P])

        id_bf = sb("id_bf", [P, P], BF16)
        maskb = sb("maskb", [P, B, P], BF16)
        tanh_g = sb("tanh_g", [P, 4])
        ctxT_hi = sb("ctxT_hi", [P, T], F32R)
        ctxT_lo = sb("ctxT_lo", [P, T], F32R)
        xn = sb("xn", [P, B, P])
        xnT = sb("xnT", [P, T])
        xnT_hi = sb("xnT_hi", [P, T], F32R)
        xnT_lo = sb("xnT_lo", [P, T], F32R)
        stats = sb("stats", [P, B, 6])
        mv = sb("mv", [P, B, 2])
        var_eps = sb("var_eps", [P, B])
        neg_half = sb("neg_half", [P, B])
        rstd = sb("rstd", [P, B])
        accT = sb("accT", [P, T])
        w_raw = sb("w_raw", [P, 768])
        b_raw = sb("b_raw", [P, 2])
        w_hi = sb("w_hi", [P, 768], F32R)
        w_lo = sb("w_lo", [P, 768], F32R)
        wo_st = sb("wo_st", [P, 2, P])
        qT = sb("qT", [P, 2, T])
        kpad = sb("kpad", [P, 2, B, 2, P])
        vpad = sb("vpad", [P, B, H4, P])
        q1f, k1f = qT[:, 0, :], qT[:, 1, :]
        q1hi = sb("q1hi", [P, T], F32R)
        q1s = sb("q1s", [P, T], F32R)
        k1hi = sb("k1hi", [P, T], F32R)
        spare = kpad[:, :, :, :, :].rearrange("p a b c k -> p (a b c k)")
        k1s = spare[:, 0:T]
        k1pad = sb("k1pad", [P, B, H4, P], F32R)
        v1_sb = spare[:, T:2 * T].rearrange("p (b d) -> p b d", b=B)
        v1pad = sb("v1pad", [P, B, H4, GR])
        nmax = sb("nmax", [P, 2, H4])
        sums = sb("sums", [P, 2, H4])
        rsum = sb("rsum", [P, 2, H4])
        probs = sb("probs", [P, 2, H4, P])
        probs_n = sb("probs_n", [P, 2, H4, P])
        probsT = sb("probsT", [P, 2, H4, P])
        oT = sb("oT", [P, 2, T])
        logit = sb("logit", [P, B, E0])
        rt = sb("rt", [P, 8, B, E0])
        rs = sb("rs", [P, 8, B])
        gate = sb("gate", [P, B, E0])
        wzero = sb("wzero", [P, B])
        gateT = sb("gateT", [E0, T])
        flat = vpad[:, :, :, :].rearrange("p b h d -> p (b h d)")
        gbc = flat[:, 0:2 * T].rearrange("p (s t) -> p s t", s=2)
        hid = flat[:, 2 * T:4 * T].rearrange("p (h c t) -> p h c t", h=2, c=C0)
        y_g = sb("y_g", [P, 2, HALF])
        gate_dram = nc.dram_tensor("gate_dram", (E0, T), F32, kind="Internal").ap()

        bank = [ctx.enter_context(nc.psum_tensor(f"bank{i}", [P, 512], F32)) for i in range(8)]
        S_BANK, T_BANK, O_BANK, M_BANK = bank[0:2], bank[2:4], bank[4:6], bank[6:8]

        def heads(b):
            return b[:, :].rearrange("p (h k) -> p h k", h=H4)

        in_x, in_ctx, in_mask, in_misc, in_w0, in_f0, in_w1, in_f1 = (
            sem(n) for n in ("in_x", "in_ctx", "in_mask", "in_misc", "in_w0", "in_f0", "in_w1", "in_f1"))
        consts = sem("consts")
        ctx_split = sem("ctx_split")
        mask_done = sem("mask_done")
        tanh_done = sem("tanh_done")
        acc_ready = sem("acc_ready")
        chain = {}
        for e in ("dve", "pool", "act"):
            chain[e] = [sem(f"{e}_order"), 0]

        ph = {}

        def phase(name, *names):
            ph[name] = {n: sem(f"{name}_{n}") for n in names}
            return ph[name]

        for n in range(4):
            phase(f"n{n}", "accT_t", "xnew", "stat", "rstd", "xn", "xnT_p", "xnT_hi", "xnT")
        for n in range(2):
            phase(f"a{n}", "w_in", "w_split", "wo_in", "b_in", "b_split", "zeros", "proj", "proj_free", "q_ready", "k_ready", "v_ready",
                  "scores", "nmax", "exp", "rsum", "probs_n", "probsT_p", "probsT",
                  "o_p", "oT", "y_p", "acc")
            phase(f"f{n}", "logit_p", "logit", "gate", "gateT_p", "gateT", "gate_out", "gbc", "w_in", "w_split", "wo_in",
                  "h_p", "hid", "y_p", "y_g", "acc", "up_p")
        fin_t, fin, stored = sem("fin_t"), sem("fin"), sem("stored")

        def link(eng, name, ins):
            c = chain[name]
            c[1] += 1
            ins.then_inc(c[0], 1)
            eng.wait_ge(c[0], c[1])

        block = ctx.enter_context(nc.Block())

        @block.sync
        def _(sp):
            sp.dma_start(x_sb[:], x.rearrange("b t d -> t b d")).then_inc(in_x, 16)
            sp.dma_start(id_sb[:], ident).then_inc(in_x, 16)
            sp.dma_start(ctx_f[:], ctxT).then_inc(in_ctx, 16)
            sp.dma_start(w_raw[:], w0[0]).then_inc(ph["a0"]["w_in"], 16)
            sp.dma_start(mask_u8[:], mask.rearrange("(a t) -> a t", a=1).to_broadcast([P, T])).then_inc(in_mask, 16)
            sp.dma_start(causal_sb[:], causal).then_inc(in_mask, 16)
            for dst, src in ((gates_in[:, 0:2], g_x.rearrange("(a t) -> a t", a=1).to_broadcast([P, 2])),
                             (gates_in[:, 2:4], g_f.rearrange("(a t) -> a t", a=1).to_broadcast([P, 2])),
                             (col[:, 0:1], bo0), (col[:, 1:2], bo1), (col[:, 2:4], lo_row),
                             (col[:, 4:8], head_row)):
                sp.dma_start(dst, src).then_inc(in_misc, 16)
            sp.dma_start(gw0_sb[:], gw0).then_inc(in_f0, 16)
            for dst, src, n in ((gb0_sb, gb0, E0), (rev0_sb, rev0, E0)):
                sp.dma_start(dst[:], src.rearrange("(a t) -> a t", a=1).to_broadcast([P, n])).then_inc(in_f0, 16)
            sp.dma_start(wv1_sb[:], wv1).then_inc(in_w1, 16)
            sp.dma_start(bv1_sb[:], bv1.rearrange("(a t) -> a t", a=1).to_broadcast([P, P])).then_inc(in_w1, 16)
            sp.dma_start(gw1_sb[:], gw1).then_inc(in_f1, 16)
            for dst, src, n in ((gb1_sb, gb1, E1), (rev1_sb, rev1, E1)):
                sp.dma_start(dst[:], src.rearrange("(a t) -> a t", a=1).to_broadcast([P, n])).then_inc(in_f1, 16)

            def row(src, i):
                return src[bass.ds(i, 1)].rearrange("a p n -> (a p) n")

            def attention_weights(a, splits, w_src, w_dst, wo_src, wo_dst, b_src=None):
                def last(i):
                    sp.wait_ge(a["y_p"], 2 * i)
                    sp.dma_start(wo_dst, row(wo_src, i)).then_inc(a["wo_in"], 16)

                with sp.Fori(0, G - 1) as i:
                    last(i)
                    sp.wait_ge(a["w_split"], splits * (i + 1))
                    sp.dma_start(w_dst, row(w_src, i + 1)).then_inc(a["w_in"], 16)
                    if b_src is not None:
                        sp.wait_ge(a["b_split"], i + 1)
                        sp.dma_start(b_raw[:], row(b_src, i + 1)).then_inc(a["b_in"], 16)
                last(G - 1)

            def expert_weights(n, splits, steps, w_src, w_dst, w2_src, w2_dst):
                f = ph[f"f{n}"]
                rows = E0 if n == 0 else E1S
                for h in range(2):
                    sp.wait_ge(f["gateT"], h + 1)
                    sp.dma_start(gate_dram[0:rows, HALF * h:HALF * (h + 1)],
                                 gateT[0:rows, HALF * h:HALF * (h + 1)]).then_inc(f["gate_out"], 16)
                sp.wait_ge(f["gate_out"], 32)

                def broadcast(e, slot):
                    if e:
                        sp.wait_ge(f["gbc"], 32 * e)
                    if n == 0:
                        sp.dma_start(gbc[:, slot, :], gate_dram[bass.ds(e, 1), :].to_broadcast([P, T])
                                     ).then_inc(f["gbc"], 32)
                    else:
                        for j in range(2):
                            sp.dma_start(gbc[F1 * j:F1 * (j + 1), slot, :],
                                         gate_dram[bass.ds(2 * e + j, 1), :].to_broadcast([F1, T])
                                         ).then_inc(f["gbc"], 16)

                broadcast(0, 0)
                broadcast(1, 1)
                for e in range(steps):
                    if e:
                        sp.wait_ge(f["y_p"], 2 * e)
                    sp.dma_start(w2_dst, w2_src[e]).then_inc(f["wo_in"], 16)
                    if e + 1 < steps:
                        sp.wait_ge(f["w_split"], splits * (e + 1))
                        sp.dma_start(w_dst, w_src[e + 1]).then_inc(f["w_in"], 16)
                    if e >= 1 and e + 1 < steps:
                        sp.wait_ge(f["y_g"], 2 * e)
                        broadcast(e + 1, (e + 1) % 2)

            wo_flat = wo_st[:, :, :].rearrange("p a n -> p (a n)")
            attention_weights(ph["a0"], 2, w0, w_raw[:], wo0, wo_flat)
            sp.wait_ge(ph["a0"]["w_split"], 2 * G)
            sp.dma_start(w_raw[:, 0:F0], f0w1[0]).then_inc(ph["f0"]["w_in"], 16)
            sp.wait_ge(ph["a0"]["y_p"], 2 * G)
            expert_weights(0, 2, E0F, f0w1, w_raw[:, 0:F0], f0w2, wo_flat)
            sp.wait_ge(ph["f0"]["w_split"], 2 * E0F)
            sp.dma_start(w_raw[:, 0:256], wqk1[0]).then_inc(ph["a1"]["w_in"], 16)
            sp.dma_start(b_raw[:], bqk1[0]).then_inc(ph["a1"]["b_in"], 16)
            sp.wait_ge(ph["a1"]["zeros"], 2)
            attention_weights(ph["a1"], 2, wqk1, w_raw[:, 0:256], wo1, wo_st[0:GR, 0, :], bqk1)
            sp.wait_ge(ph["a1"]["w_split"], 2 * G)
            sp.dma_start(w_raw[:, 0:256], f1w13[0]).then_inc(ph["f1"]["w_in"], 16)
            sp.wait_ge(ph["a1"]["y_p"], 2 * G)
            expert_weights(1, 2, C1, f1w13, w_raw[:, 0:256], f1w2, wo_st[:, 0, :])

            for b in range(B):
                sp.wait_ge(fin, b + 1)
                sp.dma_start(out[b], xn[:, b, :]).then_inc(stored, 16)
            sp.wait_ge(stored, 16 * B)

        @block.gpsimd
        def _(pool):
            nc.gpsimd.memset(neg_half[:], -0.5).then_inc(consts, 1)
            nc.gpsimd.memset(kpad[:], 0.0).then_inc(consts, 1)
            nc.gpsimd.memset(vpad[:], 0.0).then_inc(consts, 1)
            nc.gpsimd.memset(v1pad[:], 0.0).then_inc(consts, 1)
            nc.gpsimd.memset(bscale[:, 0:1], SCALE1).then_inc(consts, 1)
            nc.gpsimd.memset(bscale[:, 1:2], 1.0).then_inc(consts, 1)

            def norm(n):
                s = ph[f"n{n}"]
                for h in range(2):
                    sl = slice(HB * h, HB * (h + 1))
                    pool.wait_ge(s["stat"], h + 1)
                    link(pool, "pool", nc.gpsimd.tensor_scalar(var_eps[:, sl], mv[:, sl, 1], EPS, None, ALU.add))
                    nc.gpsimd.tensor_tensor(rstd[:, sl], var_eps[:, sl], neg_half[:, sl],
                                            ALU.pow).then_inc(s["rstd"], 1)

            def normalise(a, t0, t):
                pool.wait_ge(a["rsum"], t0 + t + 1)
                if isinstance(t0, int) and t0 + t < 2:
                    pass
                else:
                    pool.wait_ge(a["probsT_p"], t0 + t - 1)
                nc.gpsimd.tensor_tensor(probs_n[:, t % 2], probs[:, t % 2],
                                        rsum[:, t % 2, :].unsqueeze(2).to_broadcast([P, H4, P]),
                                        ALU.mult).then_inc(a["probs_n"], 1)

            norm(0)
            a = ph["a0"]

            def split_lo(s, width, i):
                pool.wait_ge(s["w_split"], 2 * i + 1)
                nc.gpsimd.tensor_tensor(w_lo[:, 0:width], w_raw[:, 0:width], w_hi[:, 0:width].bitcast(F32),
                                        ALU.subtract).then_inc(s["w_split"], 1)

            with pool.Fori(0, G) as i:
                split_lo(a, 768, i)
                for t in range(B):
                    pool.wait_ge(a["rsum"], B * i + t + 1)
                    if t >= 2:
                        pool.wait_ge(a["probsT_p"], B * i + t - 1)
                    nc.gpsimd.tensor_tensor(probs_n[:, t % 2], probs[:, t % 2],
                                            rsum[:, t % 2, :].unsqueeze(2).to_broadcast([P, H4, P]),
                                            ALU.mult).then_inc(a["probs_n"], 1)

            def experts(n, steps):
                f = ph[f"f{n}"]
                with pool.Fori(0, steps) as e:
                    split_lo(f, 256, e)
                    if n == 0:
                        for h in range(2):
                            pool.wait_ge(f["y_g"], 2 * e + h + 1)
                            nc.gpsimd.tensor_tensor(accT[:, HALF * h:HALF * (h + 1)], accT[:, HALF * h:HALF * (h + 1)],
                                                    y_g[:, h, :], ALU.add).then_inc(f["acc"], 1)

            norm(1)
            pool.wait_ge(ph["n1"]["accT_t"], B)
            nc.gpsimd.memset(accT[:], 0.0).then_inc(acc_ready, 1)
            pool.wait_ge(acc_ready, 2)
            experts(0, E0F)

            norm(2)
            a1 = ph["a1"]
            nc.gpsimd.memset(oT[:, 0, :], 0.0).then_inc(a1["zeros"], 1)
            pool.wait_ge(ph["f0"]["y_p"], 2 * E0F)
            nc.gpsimd.memset(wo_st[:, 0, :], 0.0).then_inc(a1["zeros"], 1)
            with pool.Fori(0, G) as i:
                split_lo(a1, 256, i)
                for t in range(B):
                    pool.wait_ge(a1["rsum"], B * i + t + 1)
                    if t >= 2:
                        pool.wait_ge(a1["probsT_p"], B * i + t - 1)
                    nc.gpsimd.tensor_tensor(probs_n[:, t % 2], probs[:, t % 2],
                                            rsum[:, t % 2, :].unsqueeze(2).to_broadcast([P, H4, P]),
                                            ALU.mult).then_inc(a1["probs_n"], 1)
            norm(3)
            experts(1, C1)

        @block.scalar
        def _(act):
            act.wait_ge(in_misc, 96)
            nc.scalar.activation(tanh_g[:], gates_in[:], ACT.Tanh).then_inc(tanh_done, 1)
            act.wait_ge(in_ctx, 16)
            nc.scalar.activation(ctxT_hi[:], ctx_f[:], ACT.Copy).then_inc(ctx_split, 1)
            nc.scalar.activation(accT[:], ctx_f[:], ACT.Identity, bias=col[:, 0:1], scale=0.0).then_inc(acc_ready, 1)

            def xnT_hi_copy(n):
                s = ph[f"n{n}"]
                for h in range(2):
                    act.wait_ge(s["xnT_p"], HB * (h + 1))
                    nc.scalar.activation(xnT_hi[:, HALF * h:HALF * (h + 1)], M_BANK[h][:], ACT.Copy
                                         ).then_inc(s["xnT_hi"], 1)

            def split_hi(s, width, i, used, n_used):
                act.wait_ge(used, n_used * i)
                act.wait_ge(s["w_in"], 16 * i + 16)
                nc.scalar.activation(w_hi[:, 0:width], w_raw[:, 0:width], ACT.Copy).then_inc(s["w_split"], 1)

            def softmax(a, i, t):
                act.wait_ge(a["nmax"], B * i + t + 1)
                if t >= 2:
                    act.wait_ge(a["probs_n"], B * i + t - 1)
                for h in range(H4):
                    nc.scalar.activation(probs[:, t % 2, h, :], heads(S_BANK[t % 2])[:, h, :], ACT.Exp,
                                         bias=nmax[:, t % 2, h:h + 1], accum_out=sums[:, t % 2, h:h + 1]
                                         ).then_inc(a["exp"], 1)

            xnT_hi_copy(0)
            a = ph["a0"]
            act.wait_ge(consts, 6)
            with act.Fori(0, G) as i:
                split_hi(a, 768, i, a["proj"], BANKS)
                for j in range(BANKS):
                    src = M_BANK[j % 2]
                    if j < 8:
                        if j % 2 == 1:
                            continue
                        n, p = j // 4, j // 2 % 2
                        act.wait_ge(a["proj"], BANKS * i + j + 1)
                        nc.scalar.activation(qT[:, p, HALF * n:HALF * (n + 1)], src[:], ACT.Copy, scale=SCALE0
                                             ).then_inc(a["q_ready"], 1)
                    else:
                        v = j - 8
                        act.wait_ge(a["proj"], BANKS * i + j + 1)
                        dst = vpad[:, 2 * v:2 * v + 2].rearrange("p b (c h) d -> p (b c) (h d)", h=2)
                        for hh in range(2):
                            ins = nc.scalar.activation(
                                dst[:, :, 192 * hh:192 * hh + DH0],
                                src[:].rearrange("p (m d) -> p m d", m=4)[:, :, DH0 * hh:DH0 * (hh + 1)], ACT.Copy)
                            ins.then_inc(a["v_ready"], 1)
                for t in range(B):
                    softmax(a, i, t)

            def experts(n, steps):
                f = ph[f"f{n}"]
                act.wait_ge(f["logit"], 2)
                nc.scalar.activation(rs[:, 3, :], rs[:, 2, :], ACT.Exp).then_inc(f["logit"], 1)
                for h in range(2):
                    act.wait_ge(f["gateT_p"], HB * (h + 1))
                    rows = E0 if n == 0 else E1S
                    nc.scalar.activation(gateT[0:rows, HALF * h:HALF * (h + 1)], M_BANK[h][0:rows, :], ACT.Copy
                                         ).then_inc(f["gateT"], 1)
                with act.Fori(0, steps) as e:
                    split_hi(f, 256, e, f["h_p"], 4)
                    for j in range(4):
                        if n == 1 and j % 2:
                            continue
                        act.wait_ge(f["h_p"], 4 * e + j + 1)
                        nc.scalar.activation(hid[:, j // 2, j % 2, :], bank[j][:], ACT.Silu
                                             ).then_inc(f["hid"], 1)

            def xT(n):
                xnT_hi_copy(n)

            xT(1)
            experts(0, E0F)
            xT(2)
            a = ph["a1"]
            with act.Fori(0, G) as i:
                split_hi(a, 256, i, a["proj"], 4)
                for n in range(2):
                    sl = slice(HALF * n, HALF * (n + 1))
                    act.wait_ge(a["proj"], 4 * i + 2 * n + 1)
                    act.wait_ge(a["b_split"], i + 1)
                    nc.scalar.activation(q1f[:, sl], M_BANK[0][:], ACT.Identity,
                                         bias=bqk[:, 0:1], scale=SCALE1).then_inc(a["proj_free"], 1)
                    act.wait_ge(a["proj"], 4 * i + 2 * n + 2)
                    nc.scalar.activation(k1f[:, sl], M_BANK[1][:], ACT.Identity,
                                         bias=bqk[:, 1:2]).then_inc(a["proj_free"], 1)
                for t in range(B):
                    softmax(a, i, t)
            xT(3)
            experts(1, C1)

        @block.vector
        def _(dve):
            v = nc.vector

            def layer_norm(n):
                s = ph[f"n{n}"]
                for h in range(2):
                    for b in range(HB * h, HB * (h + 1)):
                        if n > 0:
                            dve.wait_ge(s["accT_t"], HB * (h + 1))
                            p_out = T_BANK[b // HB][:, P * (b % HB):P * (b % HB + 1)]
                            g = {1: 0, 2: 2, 3: 1}[n]
                            if n == 2:
                                link(dve, "dve", v.scalar_tensor_tensor(
                                    y_g[:, 0, 0:P], xn[:, b, :], wzero[:, b:b + 1], p_out, ALU.mult, ALU.add))
                                p_out = y_g[:, 0, 0:P]
                            link(dve, "dve", v.scalar_tensor_tensor(
                                x_sb[:, b, :], p_out, tanh_g[:, g:g + 1], x_sb[:, b, :], ALU.mult, ALU.add))
                        link(dve, "dve", v.bn_stats(stats[:, b, :], x_sb[:, b, :]))
                        ins = v.bn_aggr(mv[:, b, :], stats[:, b, :])
                        if b % HB == HB - 1:
                            ins.then_inc(s["stat"], 1)
                        else:
                            link(dve, "dve", ins)
                for h in range(2):
                    dve.wait_ge(s["rstd"], h + 1)
                    for b in range(HB * h, HB * (h + 1)):
                        v.tensor_scalar(xn[:, b, :], x_sb[:, b, :], mv[:, b, 0:1], rstd[:, b:b + 1],
                                        ALU.subtract, ALU.mult).then_inc(s["xn"], 1)
                for h in range(2):
                    sl = slice(HALF * h, HALF * (h + 1))
                    dve.wait_ge(s["xnT_hi"], h + 1)
                    v.tensor_tensor(xnT_lo[:, sl], M_BANK[h][:], xnT_hi[:, sl].bitcast(F32), ALU.subtract
                                    ).then_inc(s["xnT"], 1)
                    v.tensor_copy(xnT[:, sl], M_BANK[h][:]).then_inc(s["xnT"], 1)

            def tile_max(a, i, t):
                dve.wait_ge(a["scores"], B * i + t + 1)
                v.tensor_reduce(nmax[:, t % 2, :], heads(S_BANK[t % 2]), X, ALU.max, negate=True
                                ).then_inc(a["nmax"], 1)

            def tile_rsum(a, i, t):
                dve.wait_ge(a["exp"], H4 * (B * i + t + 1))
                if t >= 2:
                    dve.wait_ge(a["probs_n"], B * i + t - 1)
                v.reciprocal(rsum[:, t % 2, :], sums[:, t % 2, :]).then_inc(a["rsum"], 1)

            def tile_probsT(a, i, t):
                dve.wait_ge(a["probsT_p"], B * i + t + 1)
                if t >= 2:
                    dve.wait_ge(a["o_p"], B * i + t - 1)
                v.tensor_copy(probsT[:, t % 2], heads(T_BANK[t % 2])).then_inc(a["probsT"], 1)

            def tile_oT(a, i, t, pairs, rows):
                dve.wait_ge(a["o_p"], B * i + t + 1)
                v.tensor_copy(oT[0:rows, 0:pairs, P * t:P * (t + 1)],
                              O_BANK[t % 2][0:rows, 0:P * pairs].rearrange("p (a q) -> p a q", a=pairs)
                              ).then_inc(a["oT"], 1)

            def attention(a, i, pairs, rows):
                for t in range(B + 3):
                    if t < B:
                        tile_max(a, i, t)
                    if 1 <= t <= B:
                        tile_rsum(a, i, t - 1)
                    if 2 <= t <= B + 1:
                        tile_probsT(a, i, t - 2)
                    if t >= 3:
                        tile_oT(a, i, t - 3, pairs, rows)
                for h in range(2):
                    sl = slice(HALF * h, HALF * (h + 1))
                    dve.wait_ge(a["y_p"], 2 * i + h + 1)
                    v.tensor_tensor(accT[:, sl], M_BANK[h][:], accT[:, sl], ALU.add).then_inc(a["acc"], 1)

            def route(n):
                f = ph[f"f{n}"]
                ne = E0 if n == 0 else E1
                gb, rev = (gb0_sb, rev0_sb) if n == 0 else (gb1_sb, rev1_sb)
                L = logit[:, :, 0:ne]
                t_ = lambda k: rt[:, k, :, 0:ne]
                wide = lambda ap: ap.unsqueeze(2).to_broadcast([P, B, ne])
                dve.wait_ge(f["logit_p"], B)
                dve.wait_ge(in_f0 if n == 0 else in_f1, 48)
                over = lambda row: row[:].unsqueeze(1).to_broadcast([P, B, ne])
                link(dve, "dve", v.tensor_tensor(
                    L, O_BANK[0][:, 0:B * ne].rearrange("p (b e) -> p b e", e=ne), over(gb), ALU.add))

                def first_best(src, best, onehot, k):
                    link(dve, "dve", v.tensor_reduce(rs[:, best, :], src, X, ALU.max))
                    link(dve, "dve", v.tensor_tensor(t_(k), src, wide(rs[:, best, :]), ALU.is_equal))
                    link(dve, "dve", v.tensor_tensor(t_(k), t_(k), over(rev), ALU.mult))
                    link(dve, "dve", v.tensor_reduce(rs[:, 7, :], t_(k), X, ALU.max))
                    link(dve, "dve", v.tensor_tensor(t_(onehot), t_(k), wide(rs[:, 7, :]), ALU.is_equal))

                first_best(L, 0, 0, 2)
                link(dve, "dve", v.scalar_tensor_tensor(t_(3), t_(0), -3.0e38, L, ALU.mult, ALU.add))
                first_best(t_(3), 1, 1, 2)
                v.tensor_tensor(rs[:, 2, :], rs[:, 1, :], rs[:, 0, :], ALU.subtract).then_inc(f["logit"], 2)
                dve.wait_ge(f["logit"], 3)
                link(dve, "dve", v.tensor_scalar(rs[:, 4, :], rs[:, 3, :], 1.0, None, ALU.add))
                link(dve, "dve", v.reciprocal(rs[:, 5, :], rs[:, 4, :]))
                link(dve, "dve", v.tensor_tensor(rs[:, 6, :], rs[:, 5, :], rs[:, 3, :], ALU.mult))
                link(dve, "dve", v.tensor_tensor(t_(4), t_(0), wide(rs[:, 5, :]), ALU.mult))
                link(dve, "dve", v.tensor_tensor(t_(5), t_(1), wide(rs[:, 6, :]), ALU.mult))
                if n == 1:
                    link(dve, "dve", v.memset(gate[:, :, E1:E1S], 1.0))
                v.tensor_tensor(gate[:, :, 0:ne], t_(4), t_(5), ALU.add).then_inc(f["gate"], 1)
                if n == 0:
                    dve.wait_ge(f["gate"], 1)
                    link(dve, "dve", v.tensor_reduce(wzero[:], gate[:, :, E0F:E0], X, ALU.add))

            def experts0():
                f = ph["f0"]
                with dve.Fori(0, E0F) as e:
                    for h in range(2):
                        sl = slice(HALF * h, HALF * (h + 1))
                        dve.wait_ge(f["y_p"], 2 * e + h + 1)
                        dve.wait_ge(f["gbc"], 32 * e + 32)
                        dve.wait_ge(f["acc"], 2 * e)
                        v.tensor_tensor(y_g[:, h, :], M_BANK[h][:], gbc_slot(e)[:, sl], ALU.mult
                                        ).then_inc(f["y_g"], 1)

            def gbc_slot(e):
                return gbc[:, bass.ds(e % 2, 1), :].rearrange("p a t -> p (a t)")

            def experts1():
                f = ph["f1"]
                with dve.Fori(0, C1) as e:
                    for h in range(2):
                        sl = slice(HALF * h, HALF * (h + 1))
                        dve.wait_ge(f["hid"], 2 * e + h + 1)
                        dve.wait_ge(f["h_p"], 4 * e + 2 * h + 2)
                        v.tensor_tensor(hid[:, h, 1, :], hid[:, h, 0, :], bank[2 * h + 1][:], ALU.mult
                                        ).then_inc(f["up_p"], 1)
                        dve.wait_ge(f["up_p"], 4 * e + 2 * h + 1)
                        dve.wait_ge(f["gbc"], 32 * e + 32)
                        v.tensor_tensor(hid[:, h, 1, :], hid[:, h, 1, :], gbc_slot(e)[:, sl], ALU.mult
                                        ).then_inc(f["up_p"], 1)
                    for h in range(2):
                        sl = slice(HALF * h, HALF * (h + 1))
                        dve.wait_ge(f["y_p"], 2 * e + h + 1)
                        v.tensor_tensor(accT[:, sl], accT[:, sl], M_BANK[h][:], ALU.add).then_inc(f["y_g"], 1)

            dve.wait_ge(in_x, 32)
            layer_norm_first = layer_norm
            v.tensor_copy(id_bf[:], id_sb[:]).then_inc(mask_done, 1)
            dve.wait_ge(in_mask, 32)
            v.scalar_tensor_tensor(maskb[:], mask_u8[:].rearrange("p (b k) -> p b k", b=B), MASKED,
                                   causal_sb[:].unsqueeze(1).to_broadcast([P, B, P]), ALU.mult, ALU.min
                                   ).then_inc(mask_done, 1)
            dve.wait_ge(ctx_split, 1)
            v.tensor_tensor(ctxT_lo[:], ctx_f[:], ctxT_hi[:].bitcast(F32), ALU.subtract).then_inc(ctx_split, 1)
            layer_norm_first(0)

            a = ph["a0"]
            dve.wait_ge(consts, 6)
            dve.wait_ge(acc_ready, 1)
            with dve.Fori(0, G) as i:
                for j in range(1, 8, 2):
                    n, p = j // 4, j // 2 % 2
                    src = M_BANK[j % 2][:].rearrange("p (b k) -> p b k", b=HB)
                    dve.wait_ge(a["proj"], BANKS * i + j + 1)
                    for hh in range(2):
                        rows = slice(DH0 * hh, DH0 * (hh + 1))
                        v.tensor_copy(kpad[rows, p, HB * n:HB * (n + 1), hh, :], src[rows]
                                      ).then_inc(a["k_ready"], 1)
                attention(a, i, 2, P)
            dve.wait_ge(tanh_done, 1)
            layer_norm(1)
            route(0)
            experts0()
            a = ph["a1"]
            dve.wait_ge(ph["f0"]["acc"], 2 * E0F)
            layer_norm(2)
            for h in range(2):
                dve.wait_ge(a["v_ready"], HB * (h + 1))
                link(dve, "dve", v.tensor_tensor(
                    v1_sb[:, HB * h:HB * (h + 1), :], S_BANK[h][:].rearrange("p (b d) -> p b d", b=HB),
                    bv1_sb[:].unsqueeze(1).to_broadcast([P, HB, P]), ALU.add))
            dve.wait_ge(ph["n2"]["accT_t"], B)
            link(dve, "dve", v.tensor_scalar(accT[:], ctx_f[:], 0.0, col[:, 1:2], ALU.mult, ALU.add))
            with dve.Fori(0, G) as i:
                if True:
                    dve.wait_ge(a["b_in"], 16 * i + 16)
                    dve.wait_ge(a["proj_free"], 4 * i)
                    v.tensor_tensor(bqk[:], b_raw[:], bscale[:], ALU.mult).then_inc(a["b_split"], 1)
                for b in range(B):
                    for h in range(H4):
                        v.tensor_copy(v1pad[:, b, h, DH1 * h:DH1 * (h + 1)],
                                      v1_sb[:, b, bass.ds(GR * i + DH1 * h, DH1)]).then_inc(a["v_ready"], 1)
                for n in range(2):
                    sl = slice(HALF * n, HALF * (n + 1))
                    dve.wait_ge(a["proj_free"], 4 * i + 2 * n + 1)
                    v.tensor_copy(q1hi[:, sl], q1f[:, sl]).then_inc(a["q_ready"], 1)
                    dve.wait_ge(a["proj_free"], 4 * i + 2 * n + 2)
                    v.tensor_copy(k1hi[:, sl], k1f[:, sl]).then_inc(a["k_ready"], 1)
                    dve.wait_ge(a["q_ready"], 4 * i + 2 * n + 1)
                    v.scalar_tensor_tensor(q1s[:, sl], q1hi[:, sl].bitcast(F32), col[:, 2:3], q1f[:, sl],
                                           ALU.mult, ALU.add).then_inc(a["q_ready"], 1)
                    dve.wait_ge(a["k_ready"], 12 * i + 6 * n + 1)
                    v.scalar_tensor_tensor(k1s[:, sl], k1hi[:, sl].bitcast(F32), col[:, 3:4], k1f[:, sl],
                                           ALU.mult, ALU.add).then_inc(a["k_ready"], 1)
                    dve.wait_ge(a["k_ready"], 12 * i + 6 * n + 2)
                    for h in range(H4):
                        v.tensor_scalar(k1pad[:, HB * n:HB * (n + 1), h, :],
                                        k1s[:, sl].rearrange("p (b k) -> p b k", b=HB), col[:, 4 + h:5 + h], None,
                                        ALU.mult).then_inc(a["k_ready"], 1)
                attention(a, i, 1, GR)
            layer_norm(3)
            route(1)
            dve.wait_ge(ph["n3"]["accT_t"], B)
            link(dve, "dve", v.memset(accT[:], 0.0))
            experts1()
            for b in range(B):
                dve.wait_ge(fin_t, HB * (b // HB + 1))
                p_out = T_BANK[b // HB][:, P * (b % HB):P * (b % HB + 1)]
                v.scalar_tensor_tensor(xn[:, b, :], p_out, tanh_g[:, 3:4], x_sb[:, b, :], ALU.mult, ALU.add
                                       ).then_inc(fin, 1)

        @block.tensor
        def _(pe):
            mm = nc.tensor.matmul

            def three(out_, w, m, **kw):
                mm(out_, w[0], m[0], start=True, stop=False)
                mm(out_, w[0], m[1], start=False, stop=False)
                return mm(out_, w[1], m[0], start=False, stop=True)

            def xnT_transposes(n):
                s = ph[f"n{n}"]
                for b in range(B):
                    pe.wait_ge(s["xn"], b + 1)
                    nc.tensor.transpose(M_BANK[b // HB][:, P * (b % HB):P * (b % HB + 1)], xn[:, b, :], id_sb[:]
                                        ).then_inc(s["xnT_p"], 1)

            def acc_transposes(s):
                for b in range(B):
                    nc.tensor.transpose(T_BANK[b // HB][:, P * (b % HB):P * (b % HB + 1)],
                                        accT[:, P * b:P * (b + 1)], id_sb[:]).then_inc(s, 1)

            def scores0(a, i, t):
                if t % HB == 0:
                    n = t // HB
                    pe.wait_ge(a["q_ready"], 4 * i + 2 * n + 2)
                    pe.wait_ge(a["k_ready"], 8 * i + 4 * n + 4)
                if t >= 2:
                    pe.wait_ge(a["exp"], H4 * (B * i + t - 1))
                s = S_BANK[t % 2]
                mm(s[:].rearrange("p (h k) -> p h k", h=H4), id_bf[:],
                   maskb[:, t, :].unsqueeze(1).to_broadcast([P, H4, P]), start=True, stop=False)
                for p in range(2):
                    ins = mm(s[:, 256 * p:256 * (p + 1)], qT[:, p, P * t:P * (t + 1)],
                             kpad[:, p, t, :, :].rearrange("p h k -> p (h k)"), start=False, stop=(p == 1))
                ins.then_inc(a["scores"], 1)

            def scores1(a, i, t):
                if t % HB == 0:
                    n = t // HB
                    pe.wait_ge(a["q_ready"], 4 * i + 2 * n + 2)
                    pe.wait_ge(a["k_ready"], 12 * i + 6 * n + 6)
                if t >= 2:
                    pe.wait_ge(a["exp"], H4 * (B * i + t - 1))
                mm(S_BANK[t % 2][:], q1s[:, P * t:P * (t + 1)], k1pad[:, t].rearrange("p h k -> p (h k)"),
                   start=True, stop=True).then_inc(a["scores"], 1)

            def turn(a, i, t):
                pe.wait_ge(a["probs_n"], B * i + t + 1)
                if t >= 2:
                    pe.wait_ge(a["probsT"], B * i + t - 1)
                for h in range(H4):
                    ins = nc.tensor.transpose(heads(T_BANK[t % 2])[:, h, :], probs_n[:, t % 2, h, :], id_sb[:])
                ins.then_inc(a["probsT_p"], 1)

            def values0(a, i, t):
                if t == 0:
                    pe.wait_ge(a["v_ready"], 8 * (i + 1))
                pe.wait_ge(a["probsT"], B * i + t + 1)
                if t >= 2:
                    pe.wait_ge(a["oT"], B * i + t - 1)
                for h in range(H4):
                    ins = mm(O_BANK[t % 2][:, P * (h // 2):P * (h // 2 + 1)], vpad[:, t, h, :], probsT[:, t % 2, h, :],
                             start=(h % 2 == 0), stop=(h % 2 == 1))
                ins.then_inc(a["o_p"], 1)

            def values1(a, i, t):
                pe.wait_ge(a["probsT"], B * i + t + 1)
                if t >= 2:
                    pe.wait_ge(a["oT"], B * i + t - 1)
                if t == 0:
                    pe.wait_ge(a["v_ready"], B + 32 * (i + 1))
                for h in range(H4):
                    ins = mm(O_BANK[t % 2][0:GR, 0:P], v1pad[:, t, h, :], probsT[:, t % 2, h, :],
                             start=(h == 0), stop=(h == H4 - 1))
                ins.then_inc(a["o_p"], 1)

            def tiles(a, i, scores, values, pairs):
                for t in range(B + 2):
                    if t < B:
                        scores(a, i, t)
                    if 1 <= t <= B:
                        turn(a, i, t - 1)
                    if t >= 2:
                        values(a, i, t - 2)
                pe.wait_ge(a["oT"], B * (i + 1))
                pe.wait_ge(a["wo_in"], 16 * i + 16)
                for h in range(2):
                    for p in range(pairs):
                        ins = mm(M_BANK[h][:], wo_st[:, p, :], oT[:, p, HALF * h:HALF * (h + 1)],
                                 start=(p == 0), stop=(p == pairs - 1))
                    ins.then_inc(a["y_p"], 1)

            pe.wait_ge(in_x, 32)
            xnT_transposes(0)
            pe.wait_ge(ctx_split, 2)
            pe.wait_ge(mask_done, 2)
            pe.wait_ge(ph["n0"]["xnT"], 4)
            a = ph["a0"]
            with pe.Fori(0, G) as i:
                pe.wait_ge(a["w_split"], 2 * i + 2)
                pe.wait_ge(a["acc"], 2 * i)
                for j in range(BANKS):
                    if j >= 2:
                        k = j - 2
                        if k < 8:
                            if k % 2 == 0:
                                pe.wait_ge(a["q_ready"], 4 * i + k // 2 + 1)
                            else:
                                pe.wait_ge(a["k_ready"], 8 * i + k + 1)
                        else:
                            pe.wait_ge(a["v_ready"], 8 * i + 2 * (k - 8) + 2)
                    dst = M_BANK[j % 2]
                    if j < 8:
                        n, p, is_k = j // 4, j // 2 % 2, j % 2
                        o = 256 * is_k + P * p
                        src = (ctxT_hi, ctxT_lo) if is_k else (xnT_hi, xnT_lo)
                        three(dst[:], (w_hi[:, o:o + P], w_lo[:, o:o + P]),
                              [m[:, HALF * n:HALF * (n + 1)] for m in src]).then_inc(a["proj"], 1)
                    else:
                        for c in range(2):
                            b = 2 * (j - 8) + c
                            ins = three(dst[:, 256 * c:256 * (c + 1)],
                                        [m[:, P * b:P * (b + 1)] for m in (ctxT_hi, ctxT_lo)],
                                        (w_hi[:, 512:768], w_lo[:, 512:768]))
                        ins.then_inc(a["proj"], 1)
                tiles(a, i, scores0, values0, 2)

            def experts(n, steps):
                f = ph[f"f{n}"]
                ne = E0 if n == 0 else E1
                gw = gw0_sb if n == 0 else gw1_sb
                pe.wait_ge(in_f0 if n == 0 else in_f1, 48)
                for b in range(B):
                    mm(O_BANK[0][:, ne * b:ne * (b + 1)], xnT[:, P * b:P * (b + 1)], gw[:], start=True, stop=True
                       ).then_inc(f["logit_p"], 1)
                pe.wait_ge(f["gate"], 1)
                rows = E0 if n == 0 else E1S
                for b in range(B):
                    nc.tensor.transpose(M_BANK[b // HB][0:rows, P * (b % HB):P * (b % HB + 1)],
                                        gate[:, b, 0:rows], id_sb[:]).then_inc(f["gateT_p"], 1)
                pe.wait_ge(f["gateT"], 2)
                with pe.Fori(0, steps) as e:
                    pe.wait_ge(f["w_split"], 2 * e + 2)
                    for h in range(2):
                        for c in range(2):
                            if n == 0:
                                pe.wait_ge(f["hid"], 4 * e)
                            else:
                                pe.wait_ge(f["hid"], 2 * e)
                                pe.wait_ge(f["up_p"], 4 * e)
                            three(bank[2 * h + c][:], (w_hi[:, P * c:P * (c + 1)], w_lo[:, P * c:P * (c + 1)]),
                                  [m[:, HALF * h:HALF * (h + 1)] for m in (xnT_hi, xnT_lo)]).then_inc(f["h_p"], 1)
                    for h in range(2):
                        pe.wait_ge(f["y_g"], 2 * e)
                        if h == 0:
                            pe.wait_ge(f["wo_in"], 16 * e + 16)
                        if n == 0:
                            pe.wait_ge(f["hid"], 4 * e + 2 * h + 2)
                            for c in range(2):
                                ins = mm(M_BANK[h][:], wo_st[:, c, :], hid[:, h, c, :], start=(c == 0), stop=(c == 1))
                        else:
                            pe.wait_ge(f["up_p"], 4 * e + 2 * h + 2)
                            ins = mm(M_BANK[h][:], wo_st[:, 0, :], hid[:, h, 1, :], start=True, stop=True)
                        ins.then_inc(f["y_p"], 1)

            pe.wait_ge(a["acc"], 2 * G)
            acc_transposes(ph["n1"]["accT_t"])
            xnT_transposes(1)
            pe.wait_ge(ph["n1"]["xnT"], 4)
            experts(0, E0F)
            pe.wait_ge(in_w1, 32)
            a = ph["a1"]
            for b in range(B):
                mm(S_BANK[b // HB][:, P * (b % HB):P * (b % HB + 1)], ctx_f[:, P * b:P * (b + 1)], wv1_sb[:],
                   start=True, stop=True).then_inc(a["v_ready"], 1)
            pe.wait_ge(ph["f0"]["acc"], 2 * E0F)
            acc_transposes(ph["n2"]["accT_t"])
            xnT_transposes(2)
            pe.wait_ge(ph["n2"]["xnT"], 4)
            with pe.Fori(0, G) as i:
                pe.wait_ge(a["w_split"], 2 * i + 2)
                pe.wait_ge(a["acc"], 2 * i)
                for n in range(2):
                    for j, src in enumerate(((xnT_hi, xnT_lo), (ctxT_hi, ctxT_lo))):
                        pe.wait_ge(a["proj_free"], 4 * i + 2 * n + j - 1) if n else None
                        three(M_BANK[j][:], (w_hi[:, P * j:P * (j + 1)], w_lo[:, P * j:P * (j + 1)]),
                              [m[:, HALF * n:HALF * (n + 1)] for m in src]).then_inc(a["proj"], 1)
                tiles(a, i, scores1, values1, 1)
            pe.wait_ge(a["acc"], 2 * G)
            acc_transposes(ph["n3"]["accT_t"])
            xnT_transposes(3)
            pe.wait_ge(ph["n3"]["xnT"], 4)
            experts(1, C1)
            pe.wait_ge(ph["f1"]["y_g"], 2 * C1)
            acc_transposes(fin_t)


def kernel(**inp):
    import numpy as np
    import concourse.bacc as bacc
    from concourse.bass_utils import run_bass_kernel_spmd as run

    a = {k: np.asarray(v) for k, v in inp.items()}
    t = np.ascontiguousarray
    w0 = np.stack([a[f"L0_xattn_W{n}"].reshape(P, G, 256) for n in "qkv"], 2).reshape(P, G, 768).transpose(1, 0, 2)
    f1 = lambda n: (np.concatenate([a[f"L1_ffn_routed_{n}"], a[f"L1_ffn_shared_{n}"]])
                    .reshape(C1, 2, P, F1).transpose(0, 2, 1, 3).reshape(C1, P, P))
    w2 = np.concatenate([a["L1_ffn_routed_w2"], a["L1_ffn_shared_w2"]]).reshape(C1, P, P)
    quad = np.arange(P) // GR
    lo_row = np.stack([-(quad % 2), -(quad // 2)], 1).astype(np.float32)
    head_row = (np.arange(P)[:, None] % GR // DH1 == np.arange(H4)[None, :]).astype(np.float32)
    group = lambda bias: np.tile(bias.reshape(G, GR), (1, 4)).T
    four = lambda w: np.tile(w.reshape(G, GR, P).transpose(0, 2, 1), (1, 1, 4))
    arrays = {
        "x": a["x"], "ctxT": t(a["ctx_1024"].transpose(2, 0, 1).reshape(P, T)),
        "mask": t(a["mask_BxS2_bf0"]).reshape(T),
        "g_x": a["g_xattn"], "g_f": a["g_ffn"],
        "w0": t(w0), "wo0": t(a["L0_xattn_Wo"].reshape(G, 2, P, P).transpose(0, 2, 1, 3).reshape(G, P, 256)),
        "bo0": a["L0_xattn_bo"].reshape(P, 1),
        "gw0": t(a["L0_ffn_gate_w"].T), "gb0": a["L0_ffn_expert_bias"],
        "f0w1": t(a["L0_ffn_w1"].transpose(0, 2, 1)),
        "f0w2": t(a["L0_ffn_w2"].reshape(E0F, P, C0, P).transpose(0, 3, 2, 1).reshape(E0F, P, C0 * P)),
        "wqk1": t(np.concatenate([four(a["L1_xattn_Wq"]), four(a["L1_xattn_Wk"])], 2)),
        "bqk1": t(np.stack([group(a["L1_xattn_bq"]), group(a["L1_xattn_bk"])], 2).transpose(1, 0, 2)),
        "wv1": t(a["L1_xattn_Wv"].T), "bv1": a["L1_xattn_bv"],
        "wo1": t(a["L1_xattn_Wo"].T.reshape(G, GR, P)), "bo1": a["L1_xattn_bo"].reshape(P, 1),
        "gw1": a["L1_ffn_router_w"], "gb1": a["L1_ffn_router_b"],
        "f1w13": t(np.concatenate([f1("w1"), f1("w3")], 2)), "f1w2": w2,
        "ident": np.eye(P, dtype=np.float32),
        "causal": np.where(np.arange(P)[None, :] > np.arange(P)[:, None], MASKED, 0.0).astype(np.float32),
        "lo_row": lo_row, "head_row": head_row,
        "rev0": np.arange(E0, 0, -1).astype(np.float32), "rev1": np.arange(E1, 0, -1).astype(np.float32),
    }
    nc = bacc.Bacc("TRN2", target_bir_lowering=False, num_devices=1)
    args = {k: nc.dram_tensor(f"in_{k}", v.shape, mybir.dt.from_np(v.dtype), kind="ExternalInput").ap()
            for k, v in arrays.items()}
    out = nc.dram_tensor("out_x", (B, P, P), F32, kind="ExternalOutput").ap()
    build(nc, out=out, **args)
    r = run(nc, [{f"in_{k}": v for k, v in arrays.items()}], core_ids=[0])
    return r.results[0]["out_x"]
```

```python
from contextlib import ExitStack

import concourse.bass as bass
from concourse import mybir

F32 = mybir.dt.float32
F32R = mybir.dt.float32r
BF16 = mybir.dt.bfloat16
U8 = mybir.dt.uint8
ALU = mybir.AluOpType
ACT = mybir.ActivationFunctionType
X = mybir.AxisListType.X

P = 128
B = 8
T = B * P
HALF = T // 2
HB = B // 2
H4 = 4
G = 4
DH0 = 64
SCALE0 = DH0 ** -0.5
DH1 = 8
SCALE1 = DH1 ** -0.5
GR = H4 * DH1
E0, E0F, F0 = 12, 8, 256
E1, E1S = 8, 10
F1 = 64
C0 = F0 // P
C1 = E1S * F1 // P
MASKED = -float(2 ** 100)
EPS = 1e-5
N0 = 6
N1 = 2


def build(nc, x, ctxT, mask, g_x, g_f, w0, wo0, bo0, gw0, gb0, f0w1, f0w2,
          wqk1, bqk1, wv1, bv1, wo1, bo1, gw1, gb1, f1w13, f1w2,
          ident, causal, lo_row, head_row, rev0, rev1, out):
    with ExitStack() as ctx:
        def sb(name, shape, dt=F32):
            return ctx.enter_context(nc.sbuf_tensor(name, shape, dt))

        def sem(name):
            return ctx.enter_context(nc.semaphore(name))

        x_sb = sb("x_sb", [P, B, P])
        ctx_f = sb("ctx_f", [P, T])
        mask_u8 = sb("mask_u8", [P, T], U8)
        gates_in = sb("gates_in", [P, 4])
        col = sb("col", [P, 8])
        gw_sb = [sb("gw0_sb", [P, E0]), sb("gw1_sb", [P, E1])]
        gb_sb = [sb("gb0_sb", [P, E0]), sb("gb1_sb", [P, E1])]
        rev_sb = [sb("rev0_sb", [P, E0]), sb("rev1_sb", [P, E1])]
        wv1_sb = sb("wv1_sb", [P, P])
        bv1_sb = sb("bv1_sb", [P, P])
        id_sb = sb("id_sb", [P, P])
        causal_sb = sb("causal_sb", [P, P])

        id_bf = sb("id_bf", [P, P], BF16)
        maskb = sb("maskb", [P, B, P], BF16)
        tanh_g = sb("tanh_g", [P, 4])
        ctxT_hi = sb("ctxT_hi", [P, T], F32R)
        ctxT_lo = sb("ctxT_lo", [P, T], F32R)
        xn = sb("xn", [P, B, P])
        xz = sb("xz", [P, B, P])
        xnT = sb("xnT", [P, T])
        xnT_hi = sb("xnT_hi", [P, T], F32R)
        xnT_lo = sb("xnT_lo", [P, T], F32R)
        stats = sb("stats", [P, B, 6])
        mv = sb("mv", [P, B, 2])
        var_eps = sb("var_eps", [P, B])
        neg_half = sb("neg_half", [P, B])
        rstd = sb("rstd", [P, B])
        accT = sb("accT", [P, T])
        w_raw = sb("w_raw", [P, 768])
        w_hi = sb("w_hi", [P, 768], F32R)
        w_lo = sb("w_lo", [P, 768], F32R)
        wo_st = sb("wo_st", [P, 2, P])
        wo1_st = sb("wo1_st", [P, P])
        b_raw = sb("b_raw", [P, 2])
        bscale = sb("bscale", [P, 2])
        bqk = sb("bqk", [P, 2])
        qT = sb("qT", [P, 2, HALF])
        kpad = sb("kpad", [P, 2, HB, 2, P])
        vpad = sb("vpad", [P, HB, H4, P])
        q1f = sb("q1f", [P, HALF])
        k1f = sb("k1f", [P, HALF])
        k1s = sb("k1s", [P, HALF])
        q1hi = sb("q1hi", [P, HALF], F32R)
        k1hi = sb("k1hi", [P, HALF], F32R)
        q1s = sb("q1s", [P, HALF], F32R)
        k1pad = sb("k1pad", [P, HB, H4, P], F32R)
        v1_sb = sb("v1_sb", [P, HB, P])
        v1pad = sb("v1pad", [P, HB, H4, GR])
        nmax = sb("nmax", [P, 2, H4])
        sums = sb("sums", [P, 2, H4])
        rsum = sb("rsum", [P, 2, H4])
        probs = sb("probs", [P, 2, H4, P])
        probs_n = sb("probs_n", [P, 2, H4, P])
        probsT = sb("probsT", [P, 2, H4, P])
        oT = sb("oT", [P, 2, HALF])
        oT1 = sb("oT1", [P, HALF])
        logit = sb("logit", [P, HB, E0])
        rt = sb("rt", [P, 6, HB, E0])
        rs = sb("rs", [P, 8, HB])
        gate = sb("gate", [P, HB, E0])
        wzero = sb("wzero", [P, B])
        gateT = sb("gateT", [E0, HALF])
        gbc = [sb(f"gbc{h}", [P, E0F, HALF]) for h in range(2)]
        hid = sb("hid", [P, 2, C0, HALF])
        y_g = sb("y_g", [P, 2, HALF])
        ew_hi = sb("ew_hi", [P, 2 * E0F * P], F32R)
        ew_lo = sb("ew_lo", [P, 2 * E0F * P], F32R)
        ew_raw = gbc[1][:].rearrange("p e t -> p (e t)")
        ew2 = sb("ew2", [P, E0F, C0, P])
        gate_dram = nc.dram_tensor("gate_dram", (4, E0, HALF), F32, kind="Internal").ap()

        bank = [ctx.enter_context(nc.psum_tensor(f"bank{i}", [P, 512], F32)) for i in range(8)]
        S_BANK, T_BANK, M_BANK, O_BANK, L_BANK = bank[0:2], bank[2:4], bank[4:6], bank[6], bank[7]

        def heads(b):
            return b[:, :].rearrange("p (h k) -> p h k", h=H4)

        def half(h):
            return slice(HALF * h, HALF * (h + 1))

        def seqs(h):
            return slice(HB * h, HB * (h + 1))

        def part_of_weights(n, part):
            if part == "v":
                return slice(512, 768), at[0]["wv_split"]
            return slice(0, 512 if n == 0 else 256), at[n]["w_split"]

        def added(u):
            return u - u // E0F

        in_x, in_ctx, in_w, in_mask, in_misc, in_f0, in_w1, in_f1 = (
            sem(n) for n in ("in_x", "in_ctx", "in_w", "in_mask", "in_misc", "in_f0", "in_w1", "in_f1"))
        consts, ctx_split, mask_done, tanh_done = (
            sem(n) for n in ("consts", "ctx_split", "mask_done", "tanh_done"))
        order = {e: [sem(f"{e}_order"), 0] for e in ("dve", "pool")}

        def link(eng, name, ins):
            c = order[name]
            c[1] += 1
            ins.then_inc(c[0], 1)
            eng.wait_ge(c[0], c[1])

        def named(prefix, names):
            return {n: sem(f"{prefix}_{n}") for n in names.split()}

        ln = [named(f"n{n}", "accT_t xz res stat rstd xn xnT_p xnT_hi xnT") for n in range(4)]
        at = [named(f"a{n}", "w_in w_split wv_split wo_in b_in b_split proj q_ready k_ready v_p v_ready "
                    "scores nmax exp rsum probs_n probsT_p probsT o_p oT y_p acc "
                    "q_free k_free q_hi k_hi k_s") for n in range(2)]
        ex = [named(f"f{n}", "w_in w_hi w_lo wo_in h_p hid up y_p y_g acc "
                    "logit_p diff ediff gate gateT_p gateT gate_out gbc") for n in range(2)]
        fin_t, fin, stored = sem("fin_t"), sem("fin"), sem("stored")

        block = ctx.enter_context(nc.Block())

        @block.sync
        def _(sp):
            def spread(dst, src, n, s):
                sp.dma_start(dst, src.rearrange("(a t) -> a t", a=1).to_broadcast([P, n])).then_inc(s, 16)

            sp.dma_start(x_sb[:, seqs(0), :], x.rearrange("b t d -> t b d")[:, seqs(0), :]).then_inc(in_x, 16)
            sp.dma_start(ctx_f[:], ctxT).then_inc(in_ctx, 16)
            sp.dma_start(w_raw[:], w0[0]).then_inc(at[0]["w_in"], 16)
            sp.dma_start(id_sb[:], ident).then_inc(in_w, 16)
            spread(mask_u8[:], mask, T, in_mask)
            sp.dma_start(causal_sb[:], causal).then_inc(in_mask, 16)
            for dst, src in ((col[:, 0:1], bo0), (col[:, 1:2], bo1), (col[:, 2:4], lo_row), (col[:, 4:8], head_row)):
                sp.dma_start(dst, src).then_inc(in_misc, 16)
            spread(gates_in[:, 0:2], g_x, 2, in_misc)
            spread(gates_in[:, 2:4], g_f, 2, in_misc)
            sp.dma_start(x_sb[:, seqs(1), :], x.rearrange("b t d -> t b d")[:, seqs(1), :]).then_inc(in_f0, 16)
            sp.dma_start(gw_sb[0][:], gw0).then_inc(in_f0, 16)
            spread(gb_sb[0][:], gb0, E0, in_f0)
            spread(rev_sb[0][:], rev0, E0, in_f0)

            def row(src, i):
                return src[i] if isinstance(i, int) else src[bass.ds(i, 1)].rearrange("a p n -> (a p) n")

            def attention_weights(n, w_src, width, wo_src, wo_dst, b_src=None):
                a = at[n]

                def step(s, i, ahead):
                    if ahead is not None:
                        sp.wait_ge(a["w_split"], 2 * s + 2)
                        if n == 0:
                            sp.wait_ge(a["wv_split"], 2 * s + 2)
                        sp.dma_start(w_raw[:, 0:width], row(w_src, ahead)).then_inc(a["w_in"], 16)
                        if b_src is not None:
                            sp.wait_ge(a["b_split"], s + 1)
                            sp.dma_start(b_raw[:], row(b_src, ahead)).then_inc(a["b_in"], 16)
                    if not (isinstance(s, int) and s == 0):
                        sp.wait_ge(a["y_p"], s)
                    sp.dma_start(wo_dst, row(wo_src, i)).then_inc(a["wo_in"], 16)

                step(0, 0, 1)
                with sp.Fori(1, G - 1) as i:
                    step(i, i, i + 1)
                step(G - 1, G - 1, 0)
                with sp.Fori(0, G - 1) as i:
                    step(i + G, i, i + 1)
                step(2 * G - 1, G - 1, None)

            def expert_weights(n, w_src, w2_src):
                f, steps, width = ex[n], w_src.shape[0], w2_src.shape[2]
                if n:
                    sp.wait_ge(ex[0]["y_g"], 2 * E0F)
                sp.dma_start(ew_raw[:, 0:2 * P * steps].rearrange("p (e n) -> p e n", e=steps),
                             w_src.rearrange("e p n -> p e n")).then_inc(f["w_in"], 16)
                if n:
                    sp.wait_ge(ex[0]["y_p"], 2 * E0F)
                sp.dma_start(ew2[:, 0:steps].rearrange("p e c n -> p e (c n)")[:, :, 0:width],
                             w2_src.rearrange("e p n -> p e n")).then_inc(f["wo_in"], 16)

            expert_weights(0, f0w1, f0w2)
            attention_weights(0, w0, 768, wo0, wo_st[:].rearrange("p c n -> p (c n)"))
            sp.dma_start(wv1_sb[:], wv1).then_inc(in_w1, 16)
            spread(bv1_sb[:], bv1, P, in_w1)
            sp.dma_start(gw_sb[1][:], gw1).then_inc(in_f1, 16)
            spread(gb_sb[1][:], gb1, E1, in_f1)
            spread(rev_sb[1][:], rev1, E1, in_f1)
            sp.wait_ge(at[0]["w_split"], 4 * G)
            sp.wait_ge(at[0]["wv_split"], 4 * G)
            sp.dma_start(w_raw[:, 0:256], wqk1[0]).then_inc(at[1]["w_in"], 16)
            sp.dma_start(b_raw[:], bqk1[0]).then_inc(at[1]["b_in"], 16)
            expert_weights(1, f1w13, f1w2)
            attention_weights(1, wqk1, 256, wo1, wo1_st[0:GR, :], bqk1)
            for h in range(2):
                sp.wait_ge(fin, h + 1)
                sp.dma_start(out.rearrange("b t d -> t b d")[:, seqs(h), :], xn[:, seqs(h), :]).then_inc(stored, 16)
            sp.wait_ge(stored, 32)

        @block.gpsimd
        def _(pool):
            g = nc.gpsimd
            for dst, value in ((neg_half[:], -0.5), (kpad[:], 0.0), (vpad[:], 0.0), (v1pad[:], 0.0),
                               (oT1[:], 0.0), (wo1_st[:], 0.0), (bscale[:, 0:1], SCALE1), (bscale[:, 1:2], 1.0)):
                g.memset(dst, value).then_inc(consts, 1)

            def split_experts(n, piece):
                f, w = ex[n], (E0F if n == 0 else C1) * 2 * P // 4
                sl = slice(w * piece, w * (piece + 1))
                pool.wait_ge(f["w_hi"], piece + 1)
                g.tensor_tensor(ew_lo[:, sl], ew_raw[:, sl], ew_hi[:, sl].bitcast(F32), ALU.subtract
                                ).then_inc(f["w_lo"], 1)

            def split_lo(n, s, part):
                sl, done = part_of_weights(n, part)
                pool.wait_ge(done, 2 * s + 1)
                g.tensor_tensor(w_lo[:, sl], w_raw[:, sl], w_hi[:, sl].bitcast(F32), ALU.subtract
                                ).then_inc(done, 1)

            def norm(n, h):
                s = ln[n]
                pool.wait_ge(s["stat"], h + 1)
                if n == h == 0:
                    pool.wait_ge(consts, 8)
                link(pool, "pool", g.tensor_scalar(var_eps[:, seqs(h)], mv[:, seqs(h), 1], EPS, None, ALU.add))
                g.tensor_tensor(rstd[:, seqs(h)], var_eps[:, seqs(h)], neg_half[:, seqs(h)], ALU.pow
                                ).then_inc(s["rstd"], 1)

            def zero_experts(h):
                pool.wait_ge(ex[0]["gate"], 2 * h + 2)
                g.tensor_tensor(xz[:, seqs(h), :], xn[:, seqs(h), :],
                                wzero[:, seqs(h)].unsqueeze(2).to_broadcast([P, HB, P]), ALU.mult
                                ).then_inc(ln[2]["xz"], 1)

            def normalise(a, s, t):
                pool.wait_ge(a["rsum"], HB * s + t + 1)
                if t >= 2:
                    pool.wait_ge(a["probsT_p"], HB * s + t - 1)
                g.tensor_tensor(probs_n[:, t % 2], probs[:, t % 2],
                                rsum[:, t % 2, :].unsqueeze(2).to_broadcast([P, H4, P]), ALU.mult
                                ).then_inc(a["probs_n"], 1)

            def main(n, s, ahead, layer=None):
                for t in range(HB):
                    normalise(at[n], s, t)
                    if t == 1 and layer:
                        norm(*layer)
                    if t == 1 and ahead:
                        split_lo(n, s + 1, "kq")
                    if t == 2 and ahead and n == 0:
                        split_lo(n, s + 1, "v")

            def attention(n, layers):
                for h in range(2):
                    main(n, G * h, True, layers[h])
                    split_experts(n, 2 * h)
                    main(n, G * h + 1, True)
                    split_experts(n, 2 * h + 1)
                    if h and n == 0:
                        zero_experts(0)
                    with pool.Fori(G * h + 2, G * h + G - h) as s:
                        main(n, s, True)
                main(n, 2 * G - 1, False)

            def expert(n, u):
                f = ex[n]
                if n == 0 and u % E0F:
                    pool.wait_ge(f["y_g"], u + 1)
                    h, e = divmod(u, E0F)
                    if e > 1:
                        pool.wait_ge(f["acc"], added(u - 1))
                    g.tensor_tensor(accT[:, half(h)], accT[:, half(h)], y_g[:, u % 2, :], ALU.add
                                    ).then_inc(f["acc"], 1)

            def experts(n, hooks):
                for u in range(2 * (E0F if n == 0 else C1)):
                    expert(n, u)
                    if u in hooks:
                        hooks[u]()

            norm(0, 0)
            split_lo(0, 0, "kq")
            split_lo(0, 0, "v")
            attention(0, ((0, 1), (1, 0)))
            experts(0, {0: lambda: norm(1, 1), 5: lambda: zero_experts(1), E0F: lambda: norm(2, 0)})
            split_lo(1, 0, "kq")
            attention(1, ((2, 1), (3, 0)))
            experts(1, {0: lambda: norm(3, 1)})

        @block.scalar
        def _(act):
            sc = nc.scalar

            def split_experts(n, piece):
                f, w = ex[n], (E0F if n == 0 else C1) * 2 * P // 4
                sl = slice(w * piece, w * (piece + 1))
                act.wait_ge(f["w_in"], 16)
                if n and piece == 0:
                    act.wait_ge(ex[0]["h_p"], 4 * E0F)
                sc.activation(ew_hi[:, sl], ew_raw[:, sl], ACT.Copy).then_inc(f["w_hi"], 1)

            def split_hi(n, s, part, used):
                sl, done = part_of_weights(n, part)
                if used is not None:
                    act.wait_ge(*used)
                act.wait_ge(at[n]["w_in"], 16 * s + 16)
                sc.activation(w_hi[:, sl], w_raw[:, sl], ACT.Copy).then_inc(done, 1)

            def xnT_hi_copy(n, h):
                act.wait_ge(ln[n]["xnT_p"], h + 1)
                sc.activation(xnT_hi[:, half(h)], L_BANK[:], ACT.Copy).then_inc(ln[n]["xnT_hi"], 1)

            def softmax(a, s, t):
                act.wait_ge(a["nmax"], HB * s + t + 1)
                if t >= 2:
                    act.wait_ge(a["probs_n"], HB * s + t - 1)
                for h in range(H4):
                    sc.activation(probs[:, t % 2, h, :], heads(S_BANK[t % 2])[:, h, :], ACT.Exp,
                                  bias=nmax[:, t % 2, h:h + 1], accum_out=sums[:, t % 2, h:h + 1]
                                  ).then_inc(a["exp"], 1)

            def queries0(s, p):
                a = at[0]
                act.wait_ge(a["proj"], N0 * s + 2 * p + 2)
                sc.activation(qT[:, p, :], M_BANK[1][:], ACT.Copy, scale=SCALE0).then_inc(a["q_ready"], 1)

            def values0(s, j):
                a = at[0]
                act.wait_ge(a["proj"], N0 * s + 5 + j)
                dst = vpad[:, 2 * j:2 * j + 2].rearrange("p b (c h) d -> p (b c) (h d)", h=2)
                src = M_BANK[j][:].rearrange("p (m d) -> p m d", m=4)
                for hh in range(2):
                    sc.activation(dst[:, :, 192 * hh:192 * hh + DH0], src[:, :, DH0 * hh:DH0 * (hh + 1)], ACT.Copy
                                  ).then_inc(a["v_ready"], 1)

            def junction0(s):
                for p in range(2):
                    queries0(s, p)

            def junction1(s):
                a = at[1]
                act.wait_ge(a["proj"], N1 * s + 1)
                act.wait_ge(a["b_split"], s + 1)
                sc.activation(k1f[:], M_BANK[0][:], ACT.Identity, bias=bqk[:, 1:2]).then_inc(a["k_free"], 1)
                act.wait_ge(a["proj"], N1 * s + 2)
                sc.activation(q1f[:], M_BANK[1][:], ACT.Identity, bias=bqk[:, 0:1], scale=SCALE1
                              ).then_inc(a["q_free"], 1)

            def main(n, s, ahead, diff=None):
                a = at[n]
                for t in range(HB):
                    softmax(a, s, t)
                    if n == 0 and t < 2:
                        values0(s, t)
                    if t == 1 and diff:
                        best_difference(*diff)
                    if t == 1 and ahead:
                        split_hi(n, s + 1, "kq", (a["proj"], N0 * s + 4 if n == 0 else N1 * s + 2))
                    if t == 2 and ahead and n == 0:
                        split_hi(n, s + 1, "v", (a["proj"], N0 * s + 6))

            def best_difference(n, h):
                act.wait_ge(ex[n]["diff"], h + 1)
                sc.activation(rs[:, 3, :], rs[:, 2, :], ACT.Exp).then_inc(ex[n]["ediff"], 1)

            def gates_out(n, h):
                f, rows = ex[n], E0 if n == 0 else E1S
                act.wait_ge(f["gateT_p"], h + 1)
                if h or n:
                    prev, k = (ex[n], 16 * h) if h else (ex[0], 32)
                    act.wait_ge(prev["gate_out"], k)
                sc.activation(gateT[0:rows, :], L_BANK[0:rows, :], ACT.Copy).then_inc(f["gateT"], 1)
                act.wait_ge(f["gateT"], h + 1)
                act.dma_start(gate_dram[2 * n + h, 0:rows, :], gateT[0:rows, :]).then_inc(f["gate_out"], 16)

            def gates_in_(n, h):
                f = ex[n]
                act.wait_ge(f["gate_out"], 16 * (h + 1))
                if h:
                    act.wait_ge(f["w_lo"], 4)
                if n == 0:
                    act.dma_start(gbc[h][:], gate_dram[h:h + 1, 0:E0F, :].to_broadcast([P, E0F, HALF])
                                  ).then_inc(f["gbc"], 32)
                else:
                    rows = gate_dram[2 + h:3 + h, 0:E1S, :].rearrange("a (c j) t -> a j c t", j=2)
                    for j in range(2):
                        act.dma_start(gbc[h][F1 * j:F1 * (j + 1), 0:C1, :],
                                      rows[:, j].to_broadcast([F1, C1, HALF])).then_inc(f["gbc"], 16)

            def attention(n, junction, layers):
                for h in range(2):
                    layer, route = layers[h]
                    junction(G * h)
                    main(n, G * h, True)
                    split_experts(n, 2 * h)
                    junction(G * h + 1)
                    xnT_hi_copy(*layer)
                    main(n, G * h + 1, True, route)
                    split_experts(n, 2 * h + 1)
                    if route:
                        gates_out(*route)
                    with act.Fori(G * h + 2, G * h + G - h) as s:
                        junction(s)
                        main(n, s, True)
                junction(2 * G - 1)
                main(n, 2 * G - 1, False)
                gates_in_(n, 0)

            def expert(n, u):
                f = ex[n]
                for c in range(C0 if n == 0 else 1):
                    act.wait_ge(f["h_p"], 2 * u + c + 1)
                    if u >= 2:
                        act.wait_ge(f["y_p"], u - 1)
                    sc.activation(hid[:, u % 2, c, :], bank[2 * (u % 2) + c][:], ACT.Silu).then_inc(f["hid"], 1)

            def experts(n, hooks):
                steps = E0F if n == 0 else C1
                for u in range(2 * steps):
                    expert(n, u)
                    for hook in hooks.get(u, ()):
                        hook()

            act.wait_ge(in_ctx, 16)
            sc.activation(ctxT_hi[:], ctx_f[:], ACT.Copy).then_inc(ctx_split, 1)
            act.wait_ge(in_misc, 96)
            sc.activation(tanh_g[:], gates_in[:], ACT.Tanh).then_inc(tanh_done, 1)
            xnT_hi_copy(0, 0)
            act.wait_ge(consts, 8)
            split_hi(0, 0, "kq", None)
            split_hi(0, 0, "v", None)
            attention(0, junction0, (((0, 1), None), ((1, 0), (0, 0))))
            split_hi(1, 0, "kq", (at[0]["proj"], 2 * G * N0))
            experts(0, {2: [lambda: xnT_hi_copy(1, 1)], 3: [lambda: best_difference(0, 1)],
                        4: [lambda: gates_out(0, 1)], 5: [lambda: gates_in_(0, 1)],
                        E0F + 2: [lambda: xnT_hi_copy(2, 0)]})
            attention(1, junction1, (((2, 1), None), ((3, 0), (1, 0))))
            experts(1, {2: [lambda: xnT_hi_copy(3, 1)], 3: [lambda: best_difference(1, 1)],
                        4: [lambda: gates_out(1, 1), lambda: gates_in_(1, 1)]})

        @block.vector
        def _(dve):
            v = nc.vector

            def residual_stats(n, h):
                s = ln[n]
                if n > 0:
                    dve.wait_ge(s["accT_t"], h + 1)
                    p_out = L_BANK[:].rearrange("p (b d) -> p b d", b=HB)
                    if n == 1 and h == 0:
                        dve.wait_ge(tanh_done, 1)
                    if n == 2:
                        dve.wait_ge(s["xz"], h + 1)
                        link(dve, "dve", v.tensor_tensor(xz[:, seqs(h), :], xz[:, seqs(h), :], p_out, ALU.add))
                        p_out = xz[:, seqs(h), :]
                    g = {1: 0, 2: 2, 3: 1}[n]
                    link(dve, "dve", v.scalar_tensor_tensor(
                        x_sb[:, seqs(h), :], p_out, tanh_g[:, g:g + 1], x_sb[:, seqs(h), :], ALU.mult, ALU.add))
                for b in range(HB * h, HB * (h + 1)):
                    ins = v.bn_stats(stats[:, b, :], x_sb[:, b, :])
                link(dve, "dve", ins)
                for b in range(HB * h, HB * (h + 1)):
                    ins = v.bn_aggr(mv[:, b, :], stats[:, b, :])
                ins.then_inc(s["stat"], 1)

            def normed(n, h):
                dve.wait_ge(ln[n]["rstd"], h + 1)
                dve.wait_ge(ln[n]["stat"], h + 1)
                for b in range(HB * h, HB * (h + 1)):
                    v.tensor_scalar(xn[:, b, :], x_sb[:, b, :], mv[:, b, 0:1], rstd[:, b:b + 1],
                                    ALU.subtract, ALU.mult).then_inc(ln[n]["xn"], 1)

            def xnT_lo_copy(n, h):
                s = ln[n]
                dve.wait_ge(s["xnT_hi"], h + 1)
                v.tensor_tensor(xnT_lo[:, half(h)], L_BANK[:], xnT_hi[:, half(h)].bitcast(F32), ALU.subtract
                                ).then_inc(s["xnT"], 1)
                v.tensor_copy(xnT[:, half(h)], L_BANK[:]).then_inc(s["xnT"], 1)

            def route_best(n, h):
                f, ne = ex[n], E0 if n == 0 else E1
                t_ = lambda k: rt[:, k, :, 0:ne]
                wide = lambda ap: ap.unsqueeze(2).to_broadcast([P, HB, ne])
                over = lambda r: r[:].unsqueeze(1).to_broadcast([P, HB, ne])
                L = logit[:, :, 0:ne]
                dve.wait_ge(f["logit_p"], h + 1)
                link(dve, "dve", v.tensor_tensor(
                    L, L_BANK[:, 0:HB * ne].rearrange("p (b e) -> p b e", e=ne), over(gb_sb[n]), ALU.add))

                def first_best(src, best, onehot):
                    link(dve, "dve", v.tensor_reduce(rs[:, best, :], src, X, ALU.max))
                    link(dve, "dve", v.tensor_tensor(t_(2), src, wide(rs[:, best, :]), ALU.is_equal))
                    link(dve, "dve", v.tensor_tensor(t_(2), t_(2), over(rev_sb[n]), ALU.mult))
                    link(dve, "dve", v.tensor_reduce(rs[:, 7, :], t_(2), X, ALU.max))
                    link(dve, "dve", v.tensor_tensor(t_(onehot), t_(2), wide(rs[:, 7, :]), ALU.is_equal))

                first_best(L, 0, 0)
                link(dve, "dve", v.scalar_tensor_tensor(t_(3), t_(0), -3.0e38, L, ALU.mult, ALU.add))
                first_best(t_(3), 1, 1)
                v.tensor_tensor(rs[:, 2, :], rs[:, 1, :], rs[:, 0, :], ALU.subtract).then_inc(f["diff"], 1)

            def route_gates(n, h):
                f, ne = ex[n], E0 if n == 0 else E1
                t_ = lambda k: rt[:, k, :, 0:ne]
                wide = lambda ap: ap.unsqueeze(2).to_broadcast([P, HB, ne])
                dve.wait_ge(f["ediff"], h + 1)
                link(dve, "dve", v.tensor_scalar(rs[:, 4, :], rs[:, 3, :], 1.0, None, ALU.add))
                link(dve, "dve", v.reciprocal(rs[:, 5, :], rs[:, 4, :]))
                link(dve, "dve", v.tensor_tensor(rs[:, 6, :], rs[:, 5, :], rs[:, 3, :], ALU.mult))
                v.tensor_tensor(t_(4), t_(0), wide(rs[:, 5, :]), ALU.mult)
                link(dve, "dve", v.tensor_tensor(t_(5), t_(1), wide(rs[:, 6, :]), ALU.mult))
                if n == 1 and h == 0:
                    v.memset(gate[:, :, E1:E1S], 1.0)
                v.tensor_tensor(gate[:, :, 0:ne], t_(4), t_(5), ALU.add).then_inc(f["gate"], 1)
                if n == 0:
                    dve.wait_ge(f["gate"], 2 * h + 1)
                    v.tensor_reduce(wzero[:, seqs(h)], gate[:, :, E0F:E0], X, ALU.add).then_inc(f["gate"], 1)

            def tile_max(a, s, t):
                dve.wait_ge(a["scores"], HB * s + t + 1)
                v.tensor_reduce(nmax[:, t % 2, :], heads(S_BANK[t % 2]), X, ALU.max, negate=True
                                ).then_inc(a["nmax"], 1)

            def tile_rsum(a, s, t):
                dve.wait_ge(a["exp"], H4 * (HB * s + t + 1))
                if t >= 2:
                    dve.wait_ge(a["probs_n"], HB * s + t - 1)
                v.reciprocal(rsum[:, t % 2, :], sums[:, t % 2, :]).then_inc(a["rsum"], 1)

            def tile_probsT(a, s, t):
                dve.wait_ge(a["probsT_p"], HB * s + t + 1)
                if t >= 2:
                    dve.wait_ge(a["o_p"], HB * s + t - 1)
                v.tensor_copy(probsT[:, t % 2], heads(T_BANK[t % 2])).then_inc(a["probsT"], 1)

            def tile_oT(n, s, t):
                a = at[n]
                dve.wait_ge(a["o_p"], HB * s + t + 1)
                if n == 0:
                    v.tensor_copy(oT[:, :, P * t:P * (t + 1)], O_BANK[:, 0:2 * P].rearrange("p (a q) -> p a q", a=2)
                                  ).then_inc(a["oT"], 1)
                else:
                    v.tensor_copy(oT1[0:GR, P * t:P * (t + 1)], O_BANK[0:GR, 0:P]).then_inc(a["oT"], 1)

            def add_output(n, s, first, h):
                a = at[n]
                dve.wait_ge(a["y_p"], s + 1)
                if first:
                    v.tensor_scalar(accT[:, half(h)], M_BANK[0][:], col[:, n:n + 1], None, ALU.add).then_inc(a["acc"], 1)
                else:
                    dve.wait_ge(a["acc"], s)
                    v.tensor_tensor(accT[:, half(h)], M_BANK[0][:], accT[:, half(h)], ALU.add).then_inc(a["acc"], 1)

            def keys0(s, p):
                a = at[0]
                dve.wait_ge(a["proj"], N0 * s + 2 * p + 1)
                src = M_BANK[0][:].rearrange("p (b k) -> p b k", b=HB)
                for hh in range(2):
                    rows = slice(DH0 * hh, DH0 * (hh + 1))
                    v.tensor_copy(kpad[rows, p, :, hh, :], src[rows]).then_inc(a["k_ready"], 1)

            def tail_and_keys0(s, tail):
                a = at[0]
                if tail:
                    tile_rsum(a, s - 1, 3)
                keys0(s, 0)
                if tail:
                    tile_probsT(a, s - 1, 2)
                    tile_oT(0, s - 1, 1)
                keys0(s, 1)
                if tail:
                    tile_probsT(a, s - 1, 3)
                    tile_oT(0, s - 1, 2)
                    tile_oT(0, s - 1, 3)

            def biases1(s):
                a = at[1]
                dve.wait_ge(a["b_in"], 16 * s + 16)
                if not (isinstance(s, int) and s == 0):
                    dve.wait_ge(a["q_free"], s)
                v.tensor_tensor(bqk[:], b_raw[:], bscale[:], ALU.mult).then_inc(a["b_split"], 1)

            def tail_and_keys1(s, tail, h, group, values):
                a = at[1]
                biases1(s)
                if values:
                    dve.wait_ge(a["v_p"], h + 1)
                    if h == 0:
                        dve.wait_ge(in_w1, 32)
                    v.tensor_tensor(v1_sb[:], M_BANK[0][:].rearrange("p (b d) -> p b d", b=HB),
                                    bv1_sb[:].unsqueeze(1).to_broadcast([P, HB, P]), ALU.add
                                    ).then_inc(a["v_ready"], 1)
                if tail:
                    tile_rsum(a, s - 1, 3)
                dve.wait_ge(a["k_free"], s + 1)
                v.tensor_copy(k1hi[:], k1f[:]).then_inc(a["k_hi"], 1)
                dve.wait_ge(a["k_hi"], s + 1)
                v.scalar_tensor_tensor(k1s[:], k1hi[:].bitcast(F32), col[:, 3:4], k1f[:], ALU.mult, ALU.add
                                       ).then_inc(a["k_s"], 1)
                if tail:
                    tile_probsT(a, s - 1, 2)
                dve.wait_ge(a["k_s"], s + 1)
                for hd in range(H4):
                    v.tensor_scalar(k1pad[:, :, hd, :], k1s[:].rearrange("p (b k) -> p b k", b=HB),
                                    col[:, 4 + hd:5 + hd], None, ALU.mult).then_inc(a["k_ready"], 1)
                if tail:
                    tile_oT(1, s - 1, 1)
                dve.wait_ge(a["q_free"], s + 1)
                v.tensor_copy(q1hi[:], q1f[:]).then_inc(a["q_hi"], 1)
                if tail:
                    tile_probsT(a, s - 1, 3)
                    tile_oT(1, s - 1, 2)
                dve.wait_ge(a["q_hi"], s + 1)
                v.scalar_tensor_tensor(q1s[:], q1hi[:].bitcast(F32), col[:, 2:3], q1f[:], ALU.mult, ALU.add
                                       ).then_inc(a["q_ready"], 1)
                if values:
                    dve.wait_ge(a["v_ready"], (1 + H4 * G) * h + 1)
                if tail:
                    tile_oT(1, s - 1, 3)
                for hd in range(H4):
                    v.tensor_copy(v1pad[:, :, hd, DH1 * hd:DH1 * (hd + 1)],
                                  v1_sb[:, :, bass.ds(GR * group + DH1 * hd, DH1)]).then_inc(a["v_ready"], 1)

            def main(n, s, h, other, first, mid=(), end=()):
                a = at[n]
                tile_max(a, s, 0)
                tile_max(a, s, 1)
                tile_rsum(a, s, 0)
                tile_max(a, s, 2)
                if other is not None:
                    add_output(n, s - 1, first, other)
                tile_rsum(a, s, 1)
                for work in mid:
                    work()
                tile_probsT(a, s, 0)
                tile_max(a, s, 3)
                tile_rsum(a, s, 2)
                tile_probsT(a, s, 1)
                tile_oT(n, s, 0)
                for work in end:
                    work()

            def attention(n, layers):
                for h in range(2):
                    layer, route = layers[h]
                    junction = (lambda s, tail, group, values=False: tail_and_keys0(s, tail)) if n == 0 else (
                        lambda s, tail, group, values=False: tail_and_keys1(s, tail, h, group, values))
                    s0 = G * h
                    junction(s0, h > 0, 0, True)
                    main(n, s0, h, 0 if h else None, False,
                         mid=[lambda: residual_stats(*layer)], end=[lambda: normed(*layer)])
                    junction(s0 + 1, True, 1)
                    xnT_lo_copy(*layer)
                    main(n, s0 + 1, h, h, True,
                         mid=[lambda: route_best(*route)] if route else (),
                         end=[lambda: route_gates(*route)] if route else ())
                    with dve.Fori(2, G) as i:
                        junction(i + s0, True, i)
                        main(n, i + s0, h, h, False)
                s, a = 2 * G - 1, at[n]
                tile_rsum(a, s, 3)
                tile_probsT(a, s, 2)
                tile_oT(n, s, 1)
                tile_probsT(a, s, 3)
                tile_oT(n, s, 2)
                tile_oT(n, s, 3)
                add_output(n, s, False, 1)

            def expert0(u):
                f, h, e = ex[0], u // E0F, u % E0F
                if u in (0, E0F):
                    dve.wait_ge(f["gbc"], 32 * (h + 1))
                dve.wait_ge(f["y_p"], u + 1)
                if e == 0:
                    v.tensor_tensor(accT[:, half(h)], M_BANK[u % 2][:], gbc[h][:, e, :], ALU.mult).then_inc(f["y_g"], 1)
                else:
                    if u > 2:
                        dve.wait_ge(f["acc"], added(u - 2))
                    v.tensor_tensor(y_g[:, u % 2, :], M_BANK[u % 2][:], gbc[h][:, e, :], ALU.mult
                                    ).then_inc(f["y_g"], 1)

            def expert1_hidden(u):
                f, h, e, side = ex[1], u // C1, u % C1, u % 2
                dve.wait_ge(f["hid"], u + 1)
                dve.wait_ge(f["h_p"], 2 * u + 2)
                v.tensor_tensor(hid[:, side, 1, :], hid[:, side, 0, :], bank[2 * side + 1][:], ALU.mult
                                ).then_inc(f["up"], 1)
                if e == 0:
                    dve.wait_ge(f["gbc"], 32 * (h + 1))
                dve.wait_ge(f["up"], 2 * u + 1)
                v.tensor_tensor(hid[:, side, 1, :], hid[:, side, 1, :], gbc[h][:, e, :], ALU.mult
                                ).then_inc(f["up"], 1)

            def expert1_output(u):
                f, h, e = ex[1], u // C1, u % C1
                dve.wait_ge(f["y_p"], u + 1)
                if e == 0:
                    v.tensor_copy(accT[:, half(h)], M_BANK[u % 2][:]).then_inc(f["acc"], 1)
                else:
                    dve.wait_ge(f["acc"], u)
                    v.tensor_tensor(accT[:, half(h)], M_BANK[u % 2][:], accT[:, half(h)], ALU.add
                                    ).then_inc(f["acc"], 1)

            def finish(h):
                dve.wait_ge(fin_t, h + 1)
                v.scalar_tensor_tensor(xn[:, seqs(h), :], L_BANK[:].rearrange("p (b d) -> p b d", b=HB),
                                       tanh_g[:, 3:4], x_sb[:, seqs(h), :], ALU.mult, ALU.add).then_inc(fin, 1)

            dve.wait_ge(in_x, 16)
            residual_stats(0, 0)
            dve.wait_ge(ctx_split, 1)
            v.tensor_tensor(ctxT_lo[:], ctx_f[:], ctxT_hi[:].bitcast(F32), ALU.subtract).then_inc(ctx_split, 1)
            normed(0, 0)
            dve.wait_ge(in_w, 16)
            v.tensor_copy(id_bf[:], id_sb[:]).then_inc(mask_done, 1)
            dve.wait_ge(in_mask, 32)
            v.scalar_tensor_tensor(maskb[:], mask_u8[:].rearrange("p (b k) -> p b k", b=B), MASKED,
                                   causal_sb[:].unsqueeze(1).to_broadcast([P, B, P]), ALU.mult, ALU.min
                                   ).then_inc(mask_done, 1)
            xnT_lo_copy(0, 0)
            dve.wait_ge(consts, 8)
            dve.wait_ge(in_misc, 96)
            dve.wait_ge(in_f0, 64)
            attention(0, (((0, 1), None), ((1, 0), (0, 0))))
            hooks = {0: lambda: residual_stats(1, 1), 1: lambda: normed(1, 1), 2: lambda: xnT_lo_copy(1, 1),
                     3: lambda: (route_best(0, 1), route_gates(0, 1)),
                     E0F: lambda: residual_stats(2, 0), E0F + 1: lambda: normed(2, 0),
                     E0F + 2: lambda: xnT_lo_copy(2, 0)}
            for u in range(2 * E0F):
                expert0(u)
                if u in hooks:
                    hooks[u]()
            dve.wait_ge(in_f1, 48)
            attention(1, (((2, 1), None), ((3, 0), (1, 0))))
            hooks = {0: lambda: residual_stats(3, 1), 1: lambda: (normed(3, 1), xnT_lo_copy(3, 1)),
                     2: lambda: (route_best(1, 1), route_gates(1, 1)), C1 + 1: lambda: finish(0)}
            expert1_hidden(0)
            for u in range(2 * C1):
                if u + 1 < 2 * C1:
                    expert1_hidden(u + 1)
                expert1_output(u)
                if u in hooks:
                    hooks[u]()
            finish(1)

        @block.tensor
        def _(pe):
            mm = nc.tensor.matmul

            def three(out_, w, m):
                mm(out_, w[0], m[0], start=True, stop=False)
                mm(out_, w[0], m[1], start=False, stop=False)
                return mm(out_, w[1], m[0], start=False, stop=True)

            def four_transposes(src):
                for b in range(HB):
                    ins = nc.tensor.transpose(L_BANK[:, P * b:P * (b + 1)], src(b), id_sb[:])
                return ins

            def acc_transposes(done, h):
                four_transposes(lambda b: accT[:, HALF * h + P * b:HALF * h + P * (b + 1)]).then_inc(done, 1)

            def xn_transposes(n, h):
                pe.wait_ge(ln[n]["xn"], HB * (h + 1))
                four_transposes(lambda b: xn[:, HB * h + b, :]).then_inc(ln[n]["xnT_p"], 1)

            def logits(n, h):
                ne = E0 if n == 0 else E1
                pe.wait_ge(ln[2 * n + 1]["xnT"], 2 * (h + 1))
                for b in range(HB):
                    o = HALF * h + P * b
                    ins = mm(L_BANK[:, ne * b:ne * (b + 1)], xnT[:, o:o + P], gw_sb[n][:], start=True, stop=True)
                ins.then_inc(ex[n]["logit_p"], 1)

            def gate_transposes(n, h):
                rows = E0 if n == 0 else E1S
                pe.wait_ge(ex[n]["gate"], (2 if n == 0 else 1) * (h + 1))
                for b in range(HB):
                    ins = nc.tensor.transpose(L_BANK[0:rows, P * b:P * (b + 1)], gate[:, b, 0:rows], id_sb[:])
                ins.then_inc(ex[n]["gateT_p"], 1)

            def key_or_query0(s, h, p, j):
                a = at[0]
                if p == j == 0:
                    pe.wait_ge(a["w_split"], 2 * s + 2)
                if p:
                    pe.wait_ge(a["k_ready"], 4 * s + 2) if j == 0 else pe.wait_ge(a["q_ready"], 2 * s + 1)
                elif j == 0 and not (isinstance(s, int) and s < 2):
                    pe.wait_ge(a["acc"], s - 1)
                elif j == 1 and not (isinstance(s, int) and s == 0):
                    pe.wait_ge(a["v_ready"], 4 * s)
                if isinstance(s, int) and s % G == 0 and j == 1 and p == 0:
                    pe.wait_ge(ln[0]["xnT"], 2 * (h + 1))
                o = P * p + (0 if j else 256)
                three(M_BANK[j][:], (w_hi[:, o:o + P], w_lo[:, o:o + P]),
                      [m[:, half(h)] for m in ((xnT_hi, xnT_lo) if j else (ctxT_hi, ctxT_lo))]
                      ).then_inc(a["proj"], 1)

            def project_values0(s, h, j):
                a = at[0]
                pe.wait_ge(a["k_ready"], 4 * s + 4) if j == 0 else pe.wait_ge(a["q_ready"], 2 * s + 2)
                if j == 0:
                    pe.wait_ge(a["wv_split"], 2 * s + 2)
                for c in range(2):
                    o = HALF * h + P * (2 * j + c)
                    ins = three(M_BANK[j][:, 256 * c:256 * (c + 1)], [m[:, o:o + P] for m in (ctxT_hi, ctxT_lo)],
                                (w_hi[:, 512:768], w_lo[:, 512:768]))
                ins.then_inc(a["proj"], 1)

            def scores0(s, h, t):
                a = at[0]
                if t == 0:
                    pe.wait_ge(a["q_ready"], 2 * s + 2)
                    pe.wait_ge(a["k_ready"], 4 * s + 4)
                if t >= 2:
                    pe.wait_ge(a["exp"], H4 * (HB * s + t - 1))
                sb_ = S_BANK[t % 2]
                mm(heads(sb_), id_bf[:], maskb[:, HB * h + t, :].unsqueeze(1).to_broadcast([P, H4, P]),
                   start=True, stop=False)
                for p in range(2):
                    ins = mm(sb_[:, 256 * p:256 * (p + 1)], qT[:, p, P * t:P * (t + 1)],
                             kpad[:, p, t, :, :].rearrange("p h k -> p (h k)"), start=False, stop=(p == 1))
                ins.then_inc(a["scores"], 1)

            def scores1(s, h, t):
                a = at[1]
                if t == 0:
                    pe.wait_ge(a["q_ready"], s + 1)
                    pe.wait_ge(a["k_ready"], H4 * (s + 1))
                if t >= 2:
                    pe.wait_ge(a["exp"], H4 * (HB * s + t - 1))
                mm(S_BANK[t % 2][:], q1s[:, P * t:P * (t + 1)], k1pad[:, t].rearrange("p h k -> p (h k)"),
                   start=True, stop=True).then_inc(a["scores"], 1)

            def turn(n, s, t):
                a = at[n]
                pe.wait_ge(a["probs_n"], HB * s + t + 1)
                if t >= 2:
                    pe.wait_ge(a["probsT"], HB * s + t - 1)
                for hd in range(H4):
                    ins = nc.tensor.transpose(heads(T_BANK[t % 2])[:, hd, :], probs_n[:, t % 2, hd, :], id_sb[:])
                ins.then_inc(a["probsT_p"], 1)

            def values(n, s, t, h=None):
                a = at[n]
                if t == 0:
                    pe.wait_ge(a["v_ready"], 4 * s + 4 + (h + 1 if n else 0))
                pe.wait_ge(a["probsT"], HB * s + t + 1)
                if not (isinstance(s, int) and s == 0 and t == 0):
                    pe.wait_ge(a["oT"], HB * s + t)
                for hd in range(H4):
                    if n == 0:
                        ins = mm(O_BANK[:, P * (hd // 2):P * (hd // 2 + 1)], vpad[:, t, hd, :], probsT[:, t % 2, hd, :],
                                 start=(hd % 2 == 0), stop=(hd % 2 == 1))
                    else:
                        ins = mm(O_BANK[0:GR, 0:P], v1pad[:, t, hd, :], probsT[:, t % 2, hd, :],
                                 start=(hd == 0), stop=(hd == H4 - 1))
                ins.then_inc(a["o_p"], 1)

            def output(n, s, bank_read):
                a = at[n]
                pe.wait_ge(a["oT"], HB * (s + 1))
                pe.wait_ge(a["wo_in"], 16 * s + 16)
                pe.wait_ge(*bank_read)
                if n == 0:
                    for p in range(2):
                        ins = mm(M_BANK[0][:], wo_st[:, p, :], oT[:, p, :], start=(p == 0), stop=(p == 1))
                else:
                    ins = mm(M_BANK[0][:], wo1_st[:], oT1[:], start=True, stop=True)
                ins.then_inc(a["y_p"], 1)

            def junction0(s, h, tail, values_too=False):
                key_or_query0(s, h, 0, 0)
                if tail:
                    turn(0, s - 1, 2)
                key_or_query0(s, h, 0, 1)
                if tail:
                    values(0, s - 1, 1)
                key_or_query0(s, h, 1, 0)
                if tail:
                    turn(0, s - 1, 3)
                    values(0, s - 1, 2)
                key_or_query0(s, h, 1, 1)
                if tail:
                    values(0, s - 1, 3)

            def junction1(s, h, tail, values_too=False):
                a = at[1]
                if not (isinstance(s, int) and s < 2):
                    pe.wait_ge(a["acc"], s - 1)
                if values_too:
                    if s == 0:
                        pe.wait_ge(in_w1, 32)
                        pe.wait_ge(ex[0]["y_g"], 2 * E0F - 1)
                    for b in range(HB):
                        o = HALF * h + P * b
                        ins = mm(M_BANK[0][:, P * b:P * (b + 1)], ctx_f[:, o:o + P], wv1_sb[:], start=True, stop=True)
                    ins.then_inc(a["v_p"], 1)
                    pe.wait_ge(a["v_ready"], (1 + H4 * G) * h + 1)
                pe.wait_ge(a["w_split"], 2 * s + 2)
                for j, src in enumerate(((ctxT_hi, ctxT_lo), (xnT_hi, xnT_lo))):
                    if j and values_too:
                        pe.wait_ge(ln[2]["xnT"], 2 * (h + 1))
                        if s == 0:
                            pe.wait_ge(ex[0]["y_g"], 2 * E0F)
                    if j and not (isinstance(s, int) and s == 0):
                        pe.wait_ge(a["q_free"], s)
                    o = 0 if j else P
                    three(M_BANK[j][:], (w_hi[:, o:o + P], w_lo[:, o:o + P]), [m[:, half(h)] for m in src]
                          ).then_inc(a["proj"], 1)
                if tail:
                    turn(1, s - 1, 2)
                    values(1, s - 1, 1)
                    turn(1, s - 1, 3)
                    values(1, s - 1, 2)
                    values(1, s - 1, 3)

            def main(n, s, h, add, after_output=(), after_scores=(), end=()):
                a, scores = at[n], scores0 if n == 0 else scores1
                scores(s, h, 0)
                if n == 0:
                    project_values0(s, h, 0)
                scores(s, h, 1)
                if n == 0:
                    project_values0(s, h, 1)
                scores(s, h, 2)
                if add:
                    output(n, s - 1, (a["v_ready"], 4 * s + 2) if n == 0 else (a["k_free"], s + 1))
                for work in after_output:
                    work()
                for work in after_scores:
                    work()
                turn(n, s, 0)
                scores(s, h, 3)
                turn(n, s, 1)
                values(n, s, 0, h)
                for work in end:
                    work()

            def attention(n, layers):
                junction = junction0 if n == 0 else junction1
                for h in range(2):
                    (m, mh), route = layers[h]
                    s0 = G * h

                    def sums_back():
                        if m == 1 or m == 3:
                            pe.wait_ge(at[n]["acc"], s0)
                            if m == 3:
                                pe.wait_ge(ln[2]["xnT"], 4)
                            else:
                                pe.wait_ge(ln[0]["xnT"], 4)
                            acc_transposes(ln[m]["accT_t"], mh)
                        elif m == 2:
                            pe.wait_ge(ex[0]["acc"], added(2 * E0F - 1))
                            pe.wait_ge(ln[2]["xnT"], 2)
                            acc_transposes(ln[m]["accT_t"], mh)

                    junction(s0, h, h > 0, True)
                    main(n, s0, h, h > 0, after_scores=[sums_back])
                    junction(s0 + 1, h, True)
                    if m == 0:
                        pe.wait_ge(ln[0]["xnT"], 2)
                    xn_transposes(m, mh)
                    main(n, s0 + 1, h, True, after_output=[lambda: logits(*route)] if route else (),
                         end=[lambda: gate_transposes(*route)] if route else ())
                    with pe.Fori(2, G) as i:
                        junction(i + s0, h, True)
                        main(n, i + s0, h, True)
                s = 2 * G - 1
                turn(n, s, 2)
                values(n, s, 1)
                turn(n, s, 3)
                values(n, s, 2)
                values(n, s, 3)
                output(n, s, (at[n]["v_ready"], 4 * s + 4) if n == 0 else (at[n]["k_free"], s + 1))

            def expert_hidden(n, u):
                f, side = ex[n], u % 2
                h, e = divmod(u, E0F if n == 0 else C1)
                if u == 0:
                    pe.wait_ge(f["w_hi"], 4)
                    pe.wait_ge(f["w_lo"], 4)
                if u >= 2:
                    if n == 0:
                        pe.wait_ge(f["hid"], 2 * (u - 1))
                    else:
                        pe.wait_ge(f["up"], 2 * (u - 1))
                for c in range(2):
                    o = 2 * P * e + P * c
                    three(bank[2 * side + c][:], (ew_hi[:, o:o + P], ew_lo[:, o:o + P]),
                          [m[:, half(h)] for m in (xnT_hi, xnT_lo)]).then_inc(f["h_p"], 1)

            def expert_output(n, u):
                f, side, e = ex[n], u % 2, u % (E0F if n == 0 else C1)
                if u == 0:
                    pe.wait_ge(f["wo_in"], 16)
                if u >= 2:
                    pe.wait_ge(f["y_g"] if n == 0 else f["acc"], u - 1)
                elif u == 0:
                    pe.wait_ge(at[n]["acc"], 2 * G)
                if n == 0:
                    pe.wait_ge(f["hid"], 2 * (u + 1))
                    for c in range(C0):
                        ins = mm(M_BANK[side][:], ew2[:, e, c, :], hid[:, side, c, :],
                                 start=(c == 0), stop=(c == C0 - 1))
                else:
                    pe.wait_ge(f["up"], 2 * (u + 1))
                    ins = mm(M_BANK[side][:], ew2[:, e, 0, :], hid[:, side, 1, :], start=True, stop=True)
                ins.then_inc(f["y_p"], 1)

            def experts(n, hooks):
                steps = 2 * (E0F if n == 0 else C1)
                expert_hidden(n, 0)
                for u in range(steps):
                    if u in hooks:
                        hooks[u]()
                    if u + 1 < steps:
                        expert_hidden(n, u + 1)
                    expert_output(n, u)

            def sums_back(m, h, complete, bank_read):
                pe.wait_ge(*complete)
                pe.wait_ge(*bank_read)
                acc_transposes(ln[m]["accT_t"] if m < 4 else fin_t, h)

            pe.wait_ge(in_w, 16)
            xn_transposes(0, 0)
            pe.wait_ge(ctx_split, 2)
            pe.wait_ge(mask_done, 2)
            attention(0, (((0, 1), None), ((1, 0), (0, 0))))
            experts(0, {
                0: lambda: sums_back(1, 1, (at[0]["acc"], 2 * G), (ex[0]["gateT"], 1)),
                2: lambda: xn_transposes(1, 1),
                3: lambda: logits(0, 1),
                5: lambda: gate_transposes(0, 1),
                E0F: lambda: None,
                E0F + 1: lambda: sums_back(2, 0, (ex[0]["acc"], added(E0F - 1)), (ex[0]["gateT"], 2)),
                E0F + 2: lambda: xn_transposes(2, 0)})
            attention(1, (((2, 1), None), ((3, 0), (1, 0))))
            experts(1, {
                0: lambda: sums_back(3, 1, (at[1]["acc"], 2 * G), (ex[1]["gateT"], 1)),
                2: lambda: xn_transposes(3, 1),
                3: lambda: logits(1, 1),
                4: lambda: gate_transposes(1, 1),
                C1 + 1: lambda: sums_back(4, 0, (ex[1]["acc"], C1), (ex[1]["gateT"], 2))})
            sums_back(4, 1, (ex[1]["acc"], 2 * C1), (fin, 1))


def kernel(**inp):
    import numpy as np
    import concourse.bacc as bacc
    from concourse.bass_utils import run_bass_kernel_spmd as run

    a = {k: np.asarray(v) for k, v in inp.items()}
    t = np.ascontiguousarray
    w0 = np.stack([a[f"L0_xattn_W{n}"].reshape(P, G, 256) for n in "qkv"], 2).reshape(P, G, 768).transpose(1, 0, 2)
    f1 = lambda n: (np.concatenate([a[f"L1_ffn_routed_{n}"], a[f"L1_ffn_shared_{n}"]])
                    .reshape(C1, 2, P, F1).transpose(0, 2, 1, 3).reshape(C1, P, P))
    w2 = np.concatenate([a["L1_ffn_routed_w2"], a["L1_ffn_shared_w2"]]).reshape(C1, P, P)
    quad = np.arange(P) // GR
    lo_row = np.stack([-(quad % 2), -(quad // 2)], 1).astype(np.float32)
    head_row = (np.arange(P)[:, None] % GR // DH1 == np.arange(H4)[None, :]).astype(np.float32)
    group = lambda bias: np.tile(bias.reshape(G, GR), (1, 4)).T
    four = lambda w: np.tile(w.reshape(G, GR, P).transpose(0, 2, 1), (1, 1, 4))
    arrays = {
        "x": a["x"], "ctxT": t(a["ctx_1024"].transpose(2, 0, 1).reshape(P, T)),
        "mask": t(a["mask_BxS2_bf0"]).reshape(T),
        "g_x": a["g_xattn"], "g_f": a["g_ffn"],
        "w0": t(w0), "wo0": t(a["L0_xattn_Wo"].reshape(G, 2, P, P).transpose(0, 2, 1, 3).reshape(G, P, 256)),
        "bo0": a["L0_xattn_bo"].reshape(P, 1),
        "gw0": t(a["L0_ffn_gate_w"].T), "gb0": a["L0_ffn_expert_bias"],
        "f0w1": t(a["L0_ffn_w1"].transpose(0, 2, 1)),
        "f0w2": t(a["L0_ffn_w2"].reshape(E0F, P, C0, P).transpose(0, 3, 2, 1).reshape(E0F, P, C0 * P)),
        "wqk1": t(np.concatenate([four(a["L1_xattn_Wq"]), four(a["L1_xattn_Wk"])], 2)),
        "bqk1": t(np.stack([group(a["L1_xattn_bq"]), group(a["L1_xattn_bk"])], 2).transpose(1, 0, 2)),
        "wv1": t(a["L1_xattn_Wv"].T), "bv1": a["L1_xattn_bv"],
        "wo1": t(a["L1_xattn_Wo"].T.reshape(G, GR, P)), "bo1": a["L1_xattn_bo"].reshape(P, 1),
        "gw1": a["L1_ffn_router_w"], "gb1": a["L1_ffn_router_b"],
        "f1w13": t(np.concatenate([f1("w1"), f1("w3")], 2)), "f1w2": w2,
        "ident": np.eye(P, dtype=np.float32),
        "causal": np.where(np.arange(P)[None, :] > np.arange(P)[:, None], MASKED, 0.0).astype(np.float32),
        "lo_row": lo_row, "head_row": head_row,
        "rev0": np.arange(E0, 0, -1).astype(np.float32), "rev1": np.arange(E1, 0, -1).astype(np.float32),
    }
    nc = bacc.Bacc("TRN2", target_bir_lowering=False, num_devices=1)
    args = {k: nc.dram_tensor(f"in_{k}", v.shape, mybir.dt.from_np(v.dtype), kind="ExternalInput").ap()
            for k, v in arrays.items()}
    out = nc.dram_tensor("out_x", (B, P, P), F32, kind="ExternalOutput").ap()
    build(nc, out=out, **args)
    r = run(nc, [{f"in_{k}": v for k, v in arrays.items()}], core_ids=[0])
    return r.results[0]["out_x"]
```

```python
import math
from contextlib import ExitStack

import concourse.bass as bass
from concourse import mybir

F32 = mybir.dt.float32
F32R = mybir.dt.float32r
BF16 = mybir.dt.bfloat16
U8 = mybir.dt.uint8
ALU = mybir.AluOpType
ACT = mybir.ActivationFunctionType
X = mybir.AxisListType.X

P = 128
B = 8
T = B * P
HALF = T // 2
HB = B // 2
H4 = 4
G = 4
DH0 = 64
SCALE0 = DH0 ** -0.5
DH1 = 8
SCALE1 = DH1 ** -0.5
GR = H4 * DH1
E0, E0F, F0 = 12, 8, 256
E1, E1S = 8, 10
F1 = 64
C0 = F0 // P
C1 = E1S * F1 // P
MASKED = -float(2 ** 100)
EPS = 1e-5
N0 = 6


def build(nc, x, ctxT, mask, g_x, g_f, w0, wo0, bo0, gw0, gb0, f0w1, f0w2,
          wqk1, bqk1, wv1, bv1, wo1, bo1, gw1, gb1, f1w13, f1w2,
          ident, causal, head_row, rev0, rev1, out):
    with ExitStack() as ctx:
        def sb(name, shape, dt=F32):
            return ctx.enter_context(nc.sbuf_tensor(name, shape, dt))

        def sem(name):
            return ctx.enter_context(nc.semaphore(name))

        x_sb = sb("x_sb", [P, B, P])
        ctx_f = sb("ctx_f", [P, T])
        mask_u8 = sb("mask_u8", [P, T], U8)
        gates_in = sb("gates_in", [P, 4])
        col = sb("col", [P, 6])
        gw_sb = [sb("gw0_sb", [P, E0]), sb("gw1_sb", [P, E1])]
        gb_sb = [sb("gb0_sb", [P, E0]), sb("gb1_sb", [P, E1])]
        rev_sb = [sb("rev0_sb", [P, E0]), sb("rev1_sb", [P, E1])]
        wv1_sb = sb("wv1_sb", [P, P])
        bv1_sb = sb("bv1_sb", [P, P])
        id_sb = sb("id_sb", [P, P])
        causal_sb = sb("causal_sb", [P, P])

        id_bf = sb("id_bf", [P, P], BF16)
        maskb = sb("maskb", [P, B, P], BF16)
        tanh_g = sb("tanh_g", [P, 4])
        ctxT_hi = sb("ctxT_hi", [P, T], F32R)
        ctxT_lo = sb("ctxT_lo", [P, T], F32R)
        xn = sb("xn", [P, B, P])
        xz = sb("xz", [P, B, P])
        xnT = sb("xnT", [P, T])
        xnT_hi = sb("xnT_hi", [P, T], F32R)
        xnT_lo = sb("xnT_lo", [P, T], F32R)
        stats = sb("stats", [P, B, 6])
        mv = sb("mv", [P, B, 2])
        var_eps = sb("var_eps", [P, B])
        neg_half = sb("neg_half", [P, B])
        rstd = sb("rstd", [P, B])
        euler = sb("euler", [P, HB])
        accT = sb("accT", [P, T])
        w_raw = sb("w_raw", [P, 768])
        w_hi = sb("w_hi", [P, 768], F32R)
        w_lo = sb("w_lo", [P, 768], F32R)
        wo_st = sb("wo_st", [P, 2, P])
        wo1_st = sb("wo1_st", [P, P])
        b_raw = sb("b_raw", [P, 2])
        bscale = sb("bscale", [P, 2])
        bqk = sb("bqk", [P, 2])
        qT = sb("qT", [P, 2, HALF])
        kpad = sb("kpad", [P, 2, HB, 2, P])
        vpad = sb("vpad", [P, HB, H4, P])
        q1f, k1f = vpad[:, 0], vpad[:, 1:3]
        v1_sb = vpad[:, 3]
        v1pad = kpad[:, 0].rearrange("p a b k -> p (a b k)").rearrange("p (i b h d) -> p i b h d", i=2, b=HB, h=H4)
        q1hi = sb("q1hi", [P, HALF], F32R)
        k1hi = sb("k1hi", [P, HALF], F32R)
        q1s = sb("q1s", [P, 2, HALF], F32R)
        k1pad = sb("k1pad", [P, 2, HB, H4, P], F32R)
        nmax = sb("nmax", [P, 2, H4])
        sums = sb("sums", [P, 2, H4])
        rsum = sb("rsum", [P, 2, H4])
        probs = sb("probs", [P, 2, H4, P])
        probs_n = sb("probs_n", [P, 2, H4, P])
        probsT = sb("probsT", [P, 2, H4, P])
        oT = sb("oT", [P, 2, HALF])
        oT1 = sb("oT1", [P, HALF])
        logit = sb("logit", [P, HB, E0])
        rt = sb("rt", [P, 6, HB, E0])
        rs = sb("rs", [P, 8, HB])
        gate = sb("gate", [P, HB, E0])
        wzero = sb("wzero", [P, B])
        gateT = sb("gateT", [E0, HALF])
        gbc = [sb(f"gbc{h}", [P, E0F, HALF]) for h in range(2)]
        hid = sb("hid", [P, 2, C0, HALF])
        y_g = sb("y_g", [P, 2, HALF])
        ew_hi = sb("ew_hi", [P, 2 * E0F * P], F32R)
        ew_lo = sb("ew_lo", [P, 2 * E0F * P], F32R)
        ew_raw = gbc[1][:].rearrange("p e t -> p (e t)")
        ew2 = sb("ew2", [P, E0F, C0, P])
        gate_dram = nc.dram_tensor("gate_dram", (4, E0, HALF), F32, kind="Internal").ap()

        bank = [ctx.enter_context(nc.psum_tensor(f"bank{i}", [P, 512], F32)) for i in range(8)]
        S_BANK, T_BANK, M_BANK, O_BANK, L_BANK = bank[0:2], bank[2:4], bank[4:6], bank[6], bank[7]

        def heads(b):
            return b[:, :].rearrange("p (h k) -> p h k", h=H4)

        def half(h):
            return slice(HALF * h, HALF * (h + 1))

        def seqs(h):
            return slice(HB * h, HB * (h + 1))

        def columns1(r):
            return slice(2 * P * (r % 3), 2 * P * (r % 3 + 1))

        def part_of_weights(n, part, s):
            if part == "v":
                return slice(512, 768), at[0]["wv_split"]
            return (slice(0, 512) if n == 0 else columns1(s)), at[n]["w_split"]

        TILES1 = 2 * G * HB

        K_LO, Q_LO = slice(GR, 2 * GR), slice(2 * GR, 4 * GR)

        def by_seq(ap):
            return ap[:].rearrange("p (b k) -> p b k", b=HB)

        def bank1(r, j):
            return O_BANK if r < 2 else M_BANK[j]

        def pair1(u):
            return u if u < C1 else (u - 1) % C1

        def added(u):
            return u - u // E0F

        in_x, in_ctx, in_w, in_mask, in_misc, in_f0, in_w1, in_f1 = (
            sem(n) for n in ("in_x", "in_ctx", "in_w", "in_mask", "in_misc", "in_f0", "in_w1", "in_f1"))
        consts, ctx_hi, ctx_split, mask_done, tanh_done = (
            sem(n) for n in ("consts", "ctx_hi", "ctx_split", "mask_done", "tanh_done"))
        order = {e: [sem(f"{e}_order"), 0] for e in ("dve", "pool")}

        def link(eng, name, ins):
            c = order[name]
            c[1] += 1
            ins.then_inc(c[0], 1)
            eng.wait_ge(c[0], c[1])

        def named(prefix, names):
            return {n: sem(f"{prefix}_{n}") for n in names.split()}

        ln = [named(f"n{n}", "accT_t xz stat rstd xn xnT_p xnT_hi xnT") for n in range(4)]
        tiles = "scores nmax exp rsum probs_n probsT_p probsT o_p oT y_p acc"
        at = [named("a0", "w_in w_split wv_split wo_in proj q_ready k_ready v_ready " + tiles),
              named("a1", "w_in w_hi w_split wo_in b_in b_split k_p q_p k_free q_free k_hi q_hi k_s k_ready q_ready "
                    "v_p v_sb v_zero v_ready probsT_a " + tiles)]
        ex = [named(f"f{n}", "w_in w_hi w_lo wo_in h_p hid y_p acc logit_p diff ediff gate gateT_p gateT "
                    "gate_out " + ("up" if n else "y_g")) for n in range(2)]
        gates_back = [sem(f"gates_back{i}") for i in range(5)]
        fin_t, fin, stored = sem("fin_t"), sem("fin"), sem("stored")

        block = ctx.enter_context(nc.Block())

        @block.sync
        def _(sp):
            def spread(dst, src, n, s):
                sp.dma_start(dst, src.rearrange("(a t) -> a t", a=1).to_broadcast([P, n])).then_inc(s, 16)

            sp.dma_start(x_sb[:, seqs(0), :], x.rearrange("b t d -> t b d")[:, seqs(0), :]).then_inc(in_x, 16)
            sp.dma_start(ctx_f[:, half(0)], ctxT[:, half(0)]).then_inc(in_ctx, 16)
            sp.dma_start(w_raw[:], w0[0]).then_inc(at[0]["w_in"], 16)
            sp.dma_start(id_sb[:], ident).then_inc(in_w, 16)
            spread(mask_u8[:], mask, T, in_mask)
            sp.dma_start(causal_sb[:], causal).then_inc(in_mask, 16)
            sp.wait_ge(in_ctx, 16)
            sp.dma_start(ctx_f[:, half(1)], ctxT[:, half(1)]).then_inc(in_ctx, 16)
            for dst, src in ((col[:, 0:1], bo0), (col[:, 1:2], bo1), (col[:, 2:6], head_row)):
                sp.dma_start(dst, src).then_inc(in_misc, 16)
            spread(gates_in[:, 0:2], g_x, 2, in_misc)
            spread(gates_in[:, 2:4], g_f, 2, in_misc)
            sp.dma_start(x_sb[:, seqs(1), :], x.rearrange("b t d -> t b d")[:, seqs(1), :]).then_inc(in_f0, 16)
            sp.dma_start(gw_sb[0][:], gw0).then_inc(in_f0, 16)
            spread(gb_sb[0][:], gb0, E0, in_f0)
            spread(rev_sb[0][:], rev0, E0, in_f0)

            def row(src, i):
                return src[i] if isinstance(i, int) else src[bass.ds(i, 1)].rearrange("a p n -> (a p) n")

            def attention_weights0(w_src, width, wo_src, wo_dst):
                a = at[0]

                def step(s, i, ahead):
                    if ahead is not None:
                        sp.wait_ge(a["w_split"], 2 * s + 2)
                        sp.wait_ge(a["wv_split"], 2 * s + 2)
                        sp.dma_start(w_raw[:, 0:width], row(w_src, ahead)).then_inc(a["w_in"], 16)
                    if not (isinstance(s, int) and s == 0):
                        sp.wait_ge(a["y_p"], s)
                    sp.dma_start(wo_dst, row(wo_src, i)).then_inc(a["wo_in"], 16)

                step(0, 0, 1)
                with sp.Fori(1, G - 1) as i:
                    step(i, i, i + 1)
                step(G - 1, G - 1, 0)
                with sp.Fori(0, G - 1) as i:
                    step(i + G, i, i + 1)
                step(2 * G - 1, G - 1, None)

            def expert_weights(n, w_src, w2_src):
                f, steps, width = ex[n], w_src.shape[0], w2_src.shape[2]
                if n:
                    sp.wait_ge(ex[0]["y_g"], 2 * E0F)
                sp.dma_start(ew_raw[:, 0:2 * P * steps].rearrange("p (e n) -> p e n", e=steps),
                             w_src.rearrange("e p n -> p e n")).then_inc(f["w_in"], 16)
                if n:
                    sp.wait_ge(ex[0]["y_p"], 2 * E0F)
                sp.dma_start(ew2[:, 0:steps].rearrange("p e c n -> p e (c n)")[:, :, 0:width],
                             w2_src.rearrange("e p n -> p e n")).then_inc(f["wo_in"], 16)

            def group_weights1(r):
                a = at[1]
                if r:
                    sp.wait_ge(a["w_in"], 16 * r)
                if r > 2:
                    sp.wait_ge(a["w_split"], r - 2)
                sp.dma_start(w_raw[:, columns1(r)], wqk1[r % G]).then_inc(a["w_in"], 16)
                if r:
                    sp.wait_ge(a["b_split"], r)
                sp.dma_start(b_raw[:], bqk1[r % G]).then_inc(a["b_in"], 16)

            expert_weights(0, f0w1, f0w2)
            attention_weights0(w0, 768, wo0, wo_st[:].rearrange("p c n -> p (c n)"))
            sp.dma_start(wv1_sb[:], wv1).then_inc(in_w1, 16)
            spread(bv1_sb[:], bv1, P, in_w1)
            sp.dma_start(gw_sb[1][:], gw1).then_inc(in_f1, 16)
            spread(gb_sb[1][:], gb1, E1, in_f1)
            spread(rev_sb[1][:], rev1, E1, in_f1)
            sp.wait_ge(at[0]["w_split"], 4 * G)
            sp.wait_ge(at[0]["wv_split"], 4 * G)
            for r in range(3):
                group_weights1(r)
            expert_weights(1, f1w13, f1w2)
            for s in range(2 * G):
                if s + 3 < 2 * G:
                    group_weights1(s + 3)
                if s:
                    sp.wait_ge(at[1]["y_p"], s)
                sp.dma_start(wo1_st[0:GR, :], wo1[s % G]).then_inc(at[1]["wo_in"], 16)
            for h in range(2):
                sp.wait_ge(fin, h + 1)
                sp.dma_start(out.rearrange("b t d -> t b d")[:, seqs(h), :], xn[:, seqs(h), :]).then_inc(stored, 16)
            sp.wait_ge(stored, 32)

        @block.gpsimd
        def _(pool):
            g = nc.gpsimd
            def constants(values):
                for dst, value in values:
                    g.memset(dst, value).then_inc(consts, 1)

            def split_experts(n, piece):
                f, w = ex[n], (E0F if n == 0 else C1) * 2 * P // 4
                sl = slice(w * piece, w * (piece + 1))
                pool.wait_ge(f["w_hi"], piece + 1)
                g.tensor_tensor(ew_lo[:, sl], ew_raw[:, sl], ew_hi[:, sl].bitcast(F32), ALU.subtract
                                ).then_inc(f["w_lo"], 1)

            def split_lo(n, s, part):
                sl, done = part_of_weights(n, part, s)
                if n == 0:
                    pool.wait_ge(done, 2 * s + 1)
                else:
                    pool.wait_ge(at[1]["w_hi"], s + 1)
                g.tensor_tensor(w_lo[:, sl], w_raw[:, sl], w_hi[:, sl].bitcast(F32), ALU.subtract
                                ).then_inc(done, 1)

            def norm(n, h):
                s = ln[n]
                pool.wait_ge(s["stat"], h + 1)
                if n == h == 0:
                    pool.wait_ge(consts, 3)
                link(pool, "pool", g.tensor_scalar(var_eps[:, seqs(h)], mv[:, seqs(h), 1], EPS, None, ALU.add))
                g.tensor_tensor(rstd[:, seqs(h)], var_eps[:, seqs(h)], neg_half[:, seqs(h)], ALU.pow
                                ).then_inc(s["rstd"], 1)

            def best_difference(n, h):
                pool.wait_ge(ex[n]["diff"], h + 1)
                g.tensor_tensor(rs[:, 3, :], euler[:], rs[:, 2, :], ALU.pow).then_inc(ex[n]["ediff"], 1)

            def zero_experts(h):
                pool.wait_ge(ex[0]["gate"], 2 * h + 2)
                g.tensor_tensor(xz[:, seqs(h), :], xn[:, seqs(h), :],
                                wzero[:, seqs(h)].unsqueeze(2).to_broadcast([P, HB, P]), ALU.mult
                                ).then_inc(ln[2]["xz"], 1)

            def normalise(a, s, t, flat=False):
                pool.wait_ge(a["rsum"], HB * s + t + 1)
                if t >= 2 or flat and s:
                    pool.wait_ge(a["probsT_p"], HB * s + t - 1)
                g.tensor_tensor(probs_n[:, t % 2], probs[:, t % 2],
                                rsum[:, t % 2, :].unsqueeze(2).to_broadcast([P, H4, P]), ALU.mult
                                ).then_inc(a["probs_n"], 1)

            def main0(s, ahead, layer=None, diff=False):
                for t in range(HB):
                    normalise(at[0], s, t)
                    if t == 1 and ahead:
                        split_lo(0, s + 1, "kq")
                    if t == 2 and layer:
                        norm(*layer)
                    if t == 2 and diff:
                        best_difference(0, 0)
                    if t == 2 and ahead:
                        split_lo(0, s + 1, "v")

            def attention0(layers):
                for h in range(2):
                    main0(G * h, True, layers[h])
                    split_experts(0, 2 * h)
                    main0(G * h + 1, True, diff=h)
                    split_experts(0, 2 * h + 1)
                    if h == 0:
                        with pool.Fori(2, G) as s:
                            main0(s, True)
                main0(G + 2, True)
                zero_experts(0)
                main0(G + 3, False)

            def keys1(r):
                a = at[1]
                pool.wait_ge(a["k_hi"], r + 1)
                g.tensor_tensor(k1f[:, r % 2], k1f[:, r % 2], by_seq(k1hi).bitcast(F32), ALU.subtract
                                ).then_inc(a["k_s"], 1)

            def queries1(r):
                a = at[1]
                pool.wait_ge(a["q_hi"], r + 1)
                if r > 1:
                    pool.wait_ge(a["scores"], HB * (r - 1))
                g.tensor_tensor(by_seq(q1s[:, r % 2]), q1f, by_seq(q1hi).bitcast(F32), ALU.subtract
                                ).then_inc(a["q_ready"], 1)

            def slots1(hooks):
                for q in range(-1, TILES1):
                    s, t = divmod(q, HB)
                    if q + 1 < TILES1:
                        normalise(at[1], (q + 1) // HB, (q + 1) % HB, flat=True)
                    if q >= 0:
                        if t == 2 and s + 2 < 2 * G:
                            keys1(s + 2)
                        if t == 2 and s + 3 < 2 * G:
                            split_lo(1, s + 3, "kq")
                        if t == 3 and s + 2 < 2 * G:
                            queries1(s + 2)
                    for hook in hooks.get((s, t), ()):
                        hook()

            def expert(n, u):
                f = ex[n]
                if n == 0 and u % E0F:
                    pool.wait_ge(f["y_g"], u + 1)
                    h, e = divmod(u, E0F)
                    if e > 1:
                        pool.wait_ge(f["acc"], added(u - 1))
                    g.tensor_tensor(accT[:, half(h)], accT[:, half(h)], y_g[:, u % 2, :], ALU.add
                                    ).then_inc(f["acc"], 1)

            def experts(n, hooks):
                for u in range(2 * (E0F if n == 0 else C1)):
                    expert(n, u)
                    if u in hooks:
                        hooks[u]()

            constants(((neg_half[:], -0.5), (euler[:], math.e), (kpad[:], 0.0)))
            norm(0, 0)
            split_lo(0, 0, "kq")
            constants(((vpad[:], 0.0), (k1hi[:].bitcast(F32), 0.0), (q1hi[:].bitcast(F32), 0.0), (oT1[:], 0.0),
                       (wo1_st[:], 0.0), (bscale[:, 0:1], SCALE1), (bscale[:, 1:2], 1.0)))
            split_lo(0, 0, "v")
            attention0(((0, 1), (1, 0)))
            pool.wait_ge(at[0]["scores"], 2 * G * HB)
            g.memset(v1pad, 0.0).then_inc(at[1]["v_zero"], 1)
            split_lo(1, 0, "kq")
            experts(0, {0: lambda: norm(1, 1), 4: lambda: best_difference(0, 1), 6: lambda: zero_experts(1),
                        E0F: lambda: norm(2, 0), E0F + 1: lambda: keys1(0), E0F + 2: lambda: split_lo(1, 1, "kq"),
                        E0F + 3: lambda: split_lo(1, 2, "kq"),
                        E0F + 5: lambda: queries1(0), E0F + 6: lambda: keys1(1),
                        E0F + 7: lambda: queries1(1)})
            slots1({(0, 3): [lambda: norm(2, 1)], (0, 1): [lambda: split_experts(1, 0)],
                    (1, 1): [lambda: split_experts(1, 1)], (2, 1): [lambda: split_experts(1, 2)],
                    (3, 1): [lambda: split_experts(1, 3)], (4, 3): [lambda: norm(3, 0)],
                    (6, 2): [lambda: best_difference(1, 0)]})
            norm(3, 1)
            experts(1, {1: lambda: best_difference(1, 1)})

        @block.scalar
        def _(act):
            sc = nc.scalar

            def split_experts(n, piece):
                f, w = ex[n], (E0F if n == 0 else C1) * 2 * P // 4
                sl = slice(w * piece, w * (piece + 1))
                act.wait_ge(f["w_in"], 16)
                if n and piece == 0:
                    act.wait_ge(ex[0]["h_p"], 4 * E0F)
                sc.activation(ew_hi[:, sl], ew_raw[:, sl], ACT.Copy).then_inc(f["w_hi"], 1)

            def split_hi(n, s, part, used):
                sl, done = part_of_weights(n, part, s)
                if used is not None:
                    act.wait_ge(*used)
                act.wait_ge(at[n]["w_in"], 16 * s + 16)
                sc.activation(w_hi[:, sl], w_raw[:, sl], ACT.Copy).then_inc(done if n == 0 else at[1]["w_hi"], 1)

            def xnT_hi_copy(n, h):
                act.wait_ge(ln[n]["xnT_p"], h + 1)
                sc.activation(xnT_hi[:, half(h)], L_BANK[:], ACT.Copy).then_inc(ln[n]["xnT_hi"], 1)

            def softmax(a, s, t, flat=False):
                act.wait_ge(a["nmax"], HB * s + t + 1)
                if t >= 2 or flat and s:
                    act.wait_ge(a["probs_n"], HB * s + t - 1)
                for h in range(H4):
                    sc.activation(probs[:, t % 2, h, :], heads(S_BANK[t % 2])[:, h, :], ACT.Exp,
                                  bias=nmax[:, t % 2, h:h + 1], accum_out=sums[:, t % 2, h:h + 1]
                                  ).then_inc(a["exp"], 1)

            def queries0(s, p):
                a = at[0]
                act.wait_ge(a["proj"], N0 * s + 2 * p + 2)
                sc.activation(qT[:, p, :], M_BANK[1][:], ACT.Copy, scale=SCALE0).then_inc(a["q_ready"], 1)

            def values0(s, j):
                a = at[0]
                act.wait_ge(a["proj"], N0 * s + 5 + j)
                dst = vpad[:, 2 * j:2 * j + 2].rearrange("p b (c h) d -> p (b c) (h d)", h=2)
                src = M_BANK[j][:].rearrange("p (m d) -> p m d", m=4)
                for hh in range(2):
                    sc.activation(dst[:, :, 192 * hh:192 * hh + DH0], src[:, :, DH0 * hh:DH0 * (hh + 1)], ACT.Copy
                                  ).then_inc(a["v_ready"], 1)

            def keys1(r):
                a = at[1]
                act.wait_ge(a["k_p"], r + 1)
                if r == 0:
                    act.wait_ge(at[0]["o_p"], 2 * G * HB)
                elif r > 1:
                    act.wait_ge(a["k_ready"], H4 * (r - 1))
                act.wait_ge(a["b_split"], r + 1)
                sc.activation(k1f[:, r % 2], bank1(r, 0)[:].rearrange("p (b k) -> p b k", b=HB), ACT.Identity,
                              bias=bqk[:, 1:2]).then_inc(a["k_free"], 1)

            def queries1(r):
                a = at[1]
                act.wait_ge(a["q_p"], r + 1)
                if r:
                    act.wait_ge(a["q_ready"], r)
                sc.activation(q1f, bank1(r, 1)[:].rearrange("p (b k) -> p b k", b=HB), ACT.Identity,
                              bias=bqk[:, 0:1], scale=SCALE1).then_inc(a["q_free"], 1)

            def probsT1(s):
                a = at[1]
                act.wait_ge(a["probsT_p"], HB * s + 3)
                act.wait_ge(a["o_p"], HB * s + 1)
                sc.activation(probsT[:, 0], heads(T_BANK[0]), ACT.Copy).then_inc(a["probsT_a"], 1)

            def slots1(hooks):
                for q in range(-1, TILES1):
                    s, t = divmod(q, HB)
                    if q + 1 < TILES1:
                        softmax(at[1], (q + 1) // HB, (q + 1) % HB, True)
                    if q >= 0 and t == 0 and s + 2 < 2 * G:
                        keys1(s + 2)
                    if q >= 0:
                        if t == 2:
                            probsT1(s)
                        if t == 1 and s + 2 < 2 * G:
                            queries1(s + 2)
                            if s + 3 < 2 * G:
                                split_hi(1, s + 3, "kq", (at[1]["q_p"], s + 1))
                    for hook in hooks.get((s, t), ()):
                        hook()

            def main0(s, ahead):
                a = at[0]
                for t in range(HB):
                    softmax(a, s, t)
                    if t < 2:
                        values0(s, t)
                    if t == 1 and ahead:
                        split_hi(0, s + 1, "kq", (a["proj"], N0 * s + 4))
                    if t == 2 and ahead:
                        split_hi(0, s + 1, "v", (a["proj"], N0 * s + 6))

            def gates_out(n, h):
                f, rows = ex[n], E0 if n == 0 else E1S
                act.wait_ge(f["gateT_p"], h + 1)
                if h or n:
                    prev, k = (ex[n], 16 * h) if h else (ex[0], 32)
                    act.wait_ge(prev["gate_out"], k)
                sc.activation(gateT[0:rows, :], L_BANK[0:rows, :], ACT.Copy).then_inc(f["gateT"], 1)
                act.wait_ge(f["gateT"], h + 1)
                act.dma_start(gate_dram[2 * n + h, 0:rows, :], gateT[0:rows, :]).then_inc(f["gate_out"], 16)

            def gates_in_(n, h):
                f = ex[n]
                act.wait_ge(f["gate_out"], 16 * (h + 1))
                if h:
                    act.wait_ge(f["w_lo"], 4)
                    act.wait_ge(*((f["y_g"], E0F - 1) if n == 0 else (f["up"], 2 * (C1 - 1))))
                if n == 0:
                    for c in range(4):
                        pair = slice(2 * c, 2 * c + 2)
                        act.dma_start(gbc[h][:, pair], gate_dram[h:h + 1, pair, :].to_broadcast([P, 2, HALF])
                                      ).then_inc(gates_back[c], 16)
                else:
                    rows = gate_dram[2 + h:3 + h, 0:E1, :].rearrange("a (c j) t -> a j c t", j=2)
                    for j in range(2):
                        act.dma_start(gbc[h][F1 * j:F1 * (j + 1), 0:C1 - 1, :],
                                      rows[:, j].to_broadcast([F1, C1 - 1, HALF])).then_inc(gates_back[4], 16)

            def attention0():
                for h in range(2):
                    for p in range(2):
                        queries0(G * h, p)
                    main0(G * h, True)
                    split_experts(0, 2 * h)
                    queries0(G * h + 1, 0)
                    xnT_hi_copy(h, 1 - h)
                    queries0(G * h + 1, 1)
                    main0(G * h + 1, True)
                    split_experts(0, 2 * h + 1)
                    if h == 0:
                        with act.Fori(2, G) as s:
                            for p in range(2):
                                queries0(s, p)
                            main0(s, True)
                for s in (G + 2, G + 3):
                    queries0(s, 0)
                    queries0(s, 1)
                    main0(s, s < 2 * G - 1)
                    if s == G + 2:
                        gates_out(0, 0)
                gates_in_(0, 0)

            def expert(n, u):
                f = ex[n]
                for c in range(C0 if n == 0 else 1):
                    act.wait_ge(f["h_p"], 2 * u + c + 1)
                    if u >= 2:
                        act.wait_ge(f["y_p"], u - 1)
                    sc.activation(hid[:, u % 2, c, :], bank[2 * (u % 2) + c][:], ACT.Silu).then_inc(f["hid"], 1)

            def experts(n, hooks):
                steps = E0F if n == 0 else C1
                for u in range(2 * steps):
                    expert(n, u)
                    for hook in hooks.get(u, ()):
                        hook()

            def split_ctx(h):
                act.wait_ge(in_ctx, 16 * h + 16)
                sc.activation(ctxT_hi[:, half(h)], ctx_f[:, half(h)], ACT.Copy).then_inc(ctx_hi, 1)

            split_ctx(0)
            split_hi(0, 0, "kq", None)
            xnT_hi_copy(0, 0)
            split_hi(0, 0, "v", None)
            act.wait_ge(in_misc, 80)
            sc.activation(tanh_g[:], gates_in[:], ACT.Tanh).then_inc(tanh_done, 1)
            split_ctx(1)
            act.wait_ge(consts, 10)
            attention0()
            split_hi(1, 0, "kq", (at[0]["proj"], 2 * G * N0))
            experts(0, {3: [lambda: xnT_hi_copy(1, 1)],
                        7: [lambda: gates_out(0, 1), lambda: gates_in_(0, 1)],
                        E0F: [lambda: keys1(0)],
                        E0F + 3: [lambda: xnT_hi_copy(2, 0)],
                        E0F + 1: [lambda: split_hi(1, 1, "kq", None), lambda: split_hi(1, 2, "kq", None)],
                        E0F + 4: [lambda: queries1(0)],
                        E0F + 6: [lambda: keys1(1)],
                        E0F + 7: [lambda: queries1(1)]})
            slots1({(1, 1): [lambda: xnT_hi_copy(2, 1)], (0, 1): [lambda: split_experts(1, 0)],
                    (1, 0): [lambda: split_experts(1, 1)], (2, 0): [lambda: split_experts(1, 2)],
                    (3, 0): [lambda: split_experts(1, 3)], (5, 1): [lambda: xnT_hi_copy(3, 0)],
                    (7, 0): [lambda: gates_out(1, 0)], (7, 3): [lambda: gates_in_(1, 0)]})
            experts(1, {1: [lambda: xnT_hi_copy(3, 1)], 4: [lambda: gates_out(1, 1), lambda: gates_in_(1, 1)]})

        @block.vector
        def _(dve):
            v = nc.vector

            def residual_sum(n, h):
                s = ln[n]
                if n > 0:
                    dve.wait_ge(s["accT_t"], h + 1)
                    p_out = L_BANK[:].rearrange("p (b d) -> p b d", b=HB)
                    if n == 1 and h == 0:
                        dve.wait_ge(tanh_done, 1)
                    if n == 2:
                        dve.wait_ge(s["xz"], h + 1)
                        link(dve, "dve", v.tensor_tensor(xz[:, seqs(h), :], xz[:, seqs(h), :], p_out, ALU.add))
                        p_out = xz[:, seqs(h), :]
                    g = {1: 0, 2: 2, 3: 1}[n]
                    link(dve, "dve", v.scalar_tensor_tensor(
                        x_sb[:, seqs(h), :], p_out, tanh_g[:, g:g + 1], x_sb[:, seqs(h), :], ALU.mult, ALU.add))

            def statistics(n, h):
                for b in range(HB * h, HB * (h + 1)):
                    ins = v.bn_stats(stats[:, b, :], x_sb[:, b, :])
                link(dve, "dve", ins)
                for b in range(HB * h, HB * (h + 1)):
                    ins = v.bn_aggr(mv[:, b, :], stats[:, b, :])
                ins.then_inc(ln[n]["stat"], 1)

            def residual_stats(n, h):
                if n > 0:
                    residual_sum(n, h)
                statistics(n, h)

            def normed(n, h):
                dve.wait_ge(ln[n]["rstd"], h + 1)
                dve.wait_ge(ln[n]["stat"], h + 1)
                for b in range(HB * h, HB * (h + 1)):
                    v.tensor_scalar(xn[:, b, :], x_sb[:, b, :], mv[:, b, 0:1], rstd[:, b:b + 1],
                                    ALU.subtract, ALU.mult).then_inc(ln[n]["xn"], 1)

            def xnT_lo_copy(n, h):
                s = ln[n]
                dve.wait_ge(s["xnT_hi"], h + 1)
                v.tensor_tensor(xnT_lo[:, half(h)], L_BANK[:], xnT_hi[:, half(h)].bitcast(F32), ALU.subtract
                                ).then_inc(s["xnT"], 1)
                if n % 2:
                    v.tensor_copy(xnT[:, half(h)], L_BANK[:]).then_inc(s["xnT"], 1)

            def route_best(n, h, parts=(0, 1)):
                f, ne = ex[n], E0 if n == 0 else E1
                t_ = lambda k: rt[:, k, :, 0:ne]
                wide = lambda ap: ap.unsqueeze(2).to_broadcast([P, HB, ne])
                over = lambda r: r[:].unsqueeze(1).to_broadcast([P, HB, ne])
                L = logit[:, :, 0:ne]

                def first_best(src, best, onehot):
                    link(dve, "dve", v.tensor_reduce(rs[:, best, :], src, X, ALU.max))
                    link(dve, "dve", v.tensor_tensor(t_(2), src, wide(rs[:, best, :]), ALU.is_equal))
                    link(dve, "dve", v.tensor_tensor(t_(2), t_(2), over(rev_sb[n]), ALU.mult))
                    link(dve, "dve", v.tensor_reduce(rs[:, 7, :], t_(2), X, ALU.max))
                    link(dve, "dve", v.tensor_tensor(t_(onehot), t_(2), wide(rs[:, 7, :]), ALU.is_equal))

                if 0 in parts:
                    dve.wait_ge(f["logit_p"], h + 1)
                    link(dve, "dve", v.tensor_tensor(
                        L, L_BANK[:, 0:HB * ne].rearrange("p (b e) -> p b e", e=ne), over(gb_sb[n]), ALU.add))
                    first_best(L, 0, 0)
                if 1 in parts:
                    link(dve, "dve", v.scalar_tensor_tensor(t_(3), t_(0), -3.0e38, L, ALU.mult, ALU.add))
                    first_best(t_(3), 1, 1)
                    v.tensor_tensor(rs[:, 2, :], rs[:, 1, :], rs[:, 0, :], ALU.subtract).then_inc(f["diff"], 1)

            def route_gates(n, h):
                f, ne = ex[n], E0 if n == 0 else E1
                t_ = lambda k: rt[:, k, :, 0:ne]
                wide = lambda ap: ap.unsqueeze(2).to_broadcast([P, HB, ne])
                dve.wait_ge(f["ediff"], h + 1)
                link(dve, "dve", v.tensor_scalar(rs[:, 4, :], rs[:, 3, :], 1.0, None, ALU.add))
                link(dve, "dve", v.reciprocal(rs[:, 5, :], rs[:, 4, :]))
                link(dve, "dve", v.tensor_tensor(rs[:, 6, :], rs[:, 5, :], rs[:, 3, :], ALU.mult))
                v.tensor_tensor(t_(4), t_(0), wide(rs[:, 5, :]), ALU.mult)
                link(dve, "dve", v.tensor_tensor(t_(5), t_(1), wide(rs[:, 6, :]), ALU.mult))
                if n == 1 and h == 0:
                    v.memset(gate[:, :, E1:E1S], 1.0)
                v.tensor_tensor(gate[:, :, 0:ne], t_(4), t_(5), ALU.add).then_inc(f["gate"], 1)
                if n == 0:
                    dve.wait_ge(f["gate"], 2 * h + 1)
                    v.tensor_reduce(wzero[:, seqs(h)], gate[:, :, E0F:E0], X, ALU.add).then_inc(f["gate"], 1)

            def tile_max(a, s, t):
                dve.wait_ge(a["scores"], HB * s + t + 1)
                v.tensor_reduce(nmax[:, t % 2, :], heads(S_BANK[t % 2]), X, ALU.max, negate=True
                                ).then_inc(a["nmax"], 1)

            def tile_rsum(a, s, t, flat=False):
                dve.wait_ge(a["exp"], H4 * (HB * s + t + 1))
                if t >= 2 or flat and s:
                    dve.wait_ge(a["probs_n"], HB * s + t - 1)
                v.reciprocal(rsum[:, t % 2, :], sums[:, t % 2, :]).then_inc(a["rsum"], 1)

            def tile_probsT(a, s, t):
                dve.wait_ge(a["probsT_p"], HB * s + t + 1)
                if t >= 2:
                    dve.wait_ge(a["o_p"], HB * s + t - 1)
                v.tensor_copy(probsT[:, t % 2], heads(T_BANK[t % 2])).then_inc(a["probsT"], 1)

            def tile_probsT1(s, t):
                a = at[1]
                dve.wait_ge(a["probsT_p"], HB * s + t + 1)
                if t >= 2 or s:
                    dve.wait_ge(a["o_p"], HB * s + t - 1)
                v.tensor_copy(probsT[:, t % 2], heads(T_BANK[t % 2])).then_inc(a["probsT"], 1)

            def tile_oT(n, s, t):
                a = at[n]
                if n and s and t == 0:
                    dve.wait_ge(a["y_p"], s)
                dve.wait_ge(a["o_p"], HB * s + t + 1)
                if n == 0:
                    v.tensor_copy(oT[:, :, P * t:P * (t + 1)], O_BANK[:, 0:2 * P].rearrange("p (a q) -> p a q", a=2)
                                  ).then_inc(a["oT"], 1)
                else:
                    v.tensor_copy(oT1[0:GR, P * t:P * (t + 1)], O_BANK[0:GR, 0:P]).then_inc(a["oT"], 1)

            def add_output(n, s, first, h):
                a = at[n]
                dve.wait_ge(a["y_p"], s + 1)
                if first:
                    v.tensor_scalar(accT[:, half(h)], M_BANK[0][:], col[:, n:n + 1], None, ALU.add).then_inc(a["acc"], 1)
                else:
                    dve.wait_ge(a["acc"], s)
                    v.tensor_tensor(accT[:, half(h)], M_BANK[0][:], accT[:, half(h)], ALU.add).then_inc(a["acc"], 1)

            def keys0(s, p):
                a = at[0]
                dve.wait_ge(a["proj"], N0 * s + 2 * p + 1)
                src = M_BANK[0][:].rearrange("p (b k) -> p b k", b=HB)
                for hh in range(2):
                    rows = slice(DH0 * hh, DH0 * (hh + 1))
                    v.tensor_copy(kpad[rows, p, :, hh, :], src[rows]).then_inc(a["k_ready"], 1)

            def tail_and_keys0(s, tail, between=None):
                a = at[0]
                if tail:
                    tile_rsum(a, s - 1, 3)
                keys0(s, 0)
                if tail:
                    tile_probsT(a, s - 1, 2)
                    tile_oT(0, s - 1, 1)
                if between:
                    between()
                keys0(s, 1)
                if tail:
                    tile_probsT(a, s - 1, 3)
                    tile_oT(0, s - 1, 2)
                    tile_oT(0, s - 1, 3)

            def biases1(s):
                a = at[1]
                dve.wait_ge(a["b_in"], 16 * s + 16)
                if s:
                    dve.wait_ge(a["q_free"], s)
                v.tensor_tensor(bqk[:], b_raw[:], bscale[:], ALU.mult).then_inc(a["b_split"], 1)

            def values_all1(h):
                a = at[1]
                dve.wait_ge(a["v_p"], h + 1)
                dve.wait_ge(in_w1, 32)
                v.tensor_tensor(v1_sb, (M_BANK[1] if h else O_BANK)[:].rearrange("p (b d) -> p b d", b=HB),
                                bv1_sb[:].unsqueeze(1).to_broadcast([P, HB, P]), ALU.add).then_inc(a["v_sb"], 1)

            def values1(r):
                a = at[1]
                dve.wait_ge(a["v_sb"], r // G + 1)
                if r == 0:
                    dve.wait_ge(a["v_zero"], 1)
                if r > 1:
                    dve.wait_ge(a["o_p"], HB * (r - 1))
                for hd in range(H4):
                    c = GR * (r % G) + DH1 * hd
                    v.tensor_copy(v1pad[:, r % 2, :, hd, DH1 * hd:DH1 * (hd + 1)], v1_sb[:, :, c:c + DH1]
                                  ).then_inc(a["v_ready"], 1)

            def key_hi1(r):
                a = at[1]
                dve.wait_ge(a["k_free"], r + 1)
                if r:
                    dve.wait_ge(a["k_s"], r)
                v.tensor_copy(by_seq(k1hi)[K_LO], k1f[K_LO, r % 2]).then_inc(a["k_hi"], 1)

            def query_hi1(r):
                a = at[1]
                dve.wait_ge(a["q_free"], r + 1)
                if r:
                    dve.wait_ge(a["q_ready"], r)
                v.tensor_copy(by_seq(q1hi)[Q_LO], q1f[Q_LO]).then_inc(a["q_hi"], 1)

            def spread_keys1(r, head_pair):
                a = at[1]
                dve.wait_ge(a["k_s"], r + 1)
                if r > 1:
                    dve.wait_ge(a["scores"], HB * (r - 1))
                for hd in head_pair:
                    v.tensor_scalar(k1pad[:, r % 2, :, hd, :], k1f[:, r % 2], col[:, 2 + hd:3 + hd], None, ALU.mult
                                    ).then_inc(a["k_ready"], 1)

            def slots1(hooks):
                a = at[1]
                for q in range(-2, TILES1 + 1):
                    s, t = divmod(q, HB)
                    if q + 2 < TILES1:
                        tile_max(a, (q + 2) // HB, (q + 2) % HB)
                    if 0 <= q + 1 < TILES1:
                        tile_rsum(a, (q + 1) // HB, (q + 1) % HB, True)
                    if 0 <= q < TILES1 and t != 2:
                        tile_probsT1(s, t)
                    if q >= 0 and t == 2 and s:
                        add_output(1, s - 1, (s - 1) % G == 0, (s - 1) // G)
                    if q >= 1:
                        tile_oT(1, (q - 1) // HB, (q - 1) % HB)
                    if q >= 0:
                        ahead = s + 2 < 2 * G
                        if t == 0 and 2 <= s + 1 < 2 * G:
                            spread_keys1(s + 1, (2, 3))
                        if t == 1 and ahead:
                            key_hi1(s + 2)
                        if t == 1 and 2 <= s + 1 < 2 * G:
                            values1(s + 1)
                        if t == 2 and ahead:
                            query_hi1(s + 2)
                        if t == 3 and ahead:
                            spread_keys1(s + 2, (0, 1))
                        if t == 3 and s + 3 < 2 * G:
                            biases1(s + 3)
                        if t == 3 and s == G - 2:
                            values_all1(1)
                    for hook in hooks.get((s, t), ()):
                        hook()
                add_output(1, 2 * G - 1, False, 1)

            def main0(s, other, first, after_rsum1=None, after_rsum2=None):
                a = at[0]
                tile_max(a, s, 0)
                tile_max(a, s, 1)
                tile_rsum(a, s, 0)
                tile_max(a, s, 2)
                if other is not None:
                    add_output(0, s - 1, first, other)
                tile_rsum(a, s, 1)
                if after_rsum1:
                    after_rsum1()
                tile_probsT(a, s, 0)
                tile_max(a, s, 3)
                tile_rsum(a, s, 2)
                if after_rsum2:
                    after_rsum2()
                tile_probsT(a, s, 1)
                tile_oT(0, s, 0)

            def attention0():
                tail_and_keys0(0, False)
                split_ctx(1)
                make_mask(1)
                main0(0, None, False, after_rsum2=lambda: residual_stats(0, 1))
                tail_and_keys0(1, True, lambda: normed(0, 1))
                xnT_lo_copy(0, 1)
                main0(1, 0, True)
                with dve.Fori(2, G) as s:
                    tail_and_keys0(s, True)
                    main0(s, 0, False)
                tail_and_keys0(G, True)
                main0(G, 0, False, after_rsum2=lambda: residual_stats(1, 0))
                tail_and_keys0(G + 1, True, lambda: normed(1, 0))
                xnT_lo_copy(1, 0)
                main0(G + 1, 1, True, after_rsum1=lambda: route_best(0, 0, (0,)),
                      after_rsum2=lambda: route_best(0, 0, (1,)))
                tail_and_keys0(G + 2, True)
                main0(G + 2, 1, False, after_rsum2=lambda: route_gates(0, 0))
                tail_and_keys0(G + 3, True)
                main0(G + 3, 1, False)
                s, a = 2 * G - 1, at[0]
                tile_rsum(a, s, 3)
                tile_probsT(a, s, 2)
                tile_oT(0, s, 1)
                tile_probsT(a, s, 3)
                tile_oT(0, s, 2)
                tile_oT(0, s, 3)
                add_output(0, s, False, 1)

            def expert0(u):
                f, h, e = ex[0], u // E0F, u % E0F
                if e % 2 == 0:
                    dve.wait_ge(gates_back[e // 2], 16 * (h + 1))
                dve.wait_ge(f["y_p"], u + 1)
                if e == 0:
                    v.tensor_tensor(accT[:, half(h)], M_BANK[u % 2][:], gbc[h][:, e, :], ALU.mult).then_inc(f["y_g"], 1)
                else:
                    if u > 2:
                        dve.wait_ge(f["acc"], added(u - 2))
                    v.tensor_tensor(y_g[:, u % 2, :], M_BANK[u % 2][:], gbc[h][:, e, :], ALU.mult
                                    ).then_inc(f["y_g"], 1)

            def expert1_hidden(u):
                f, h, e, side = ex[1], u // C1, pair1(u), u % 2
                dve.wait_ge(f["hid"], u + 1)
                dve.wait_ge(f["h_p"], 2 * u + 2)
                up = v.tensor_tensor(hid[:, side, 1, :], hid[:, side, 0, :], bank[2 * side + 1][:], ALU.mult)
                if e == C1 - 1:
                    up.then_inc(f["up"], 2)
                else:
                    up.then_inc(f["up"], 1)
                    dve.wait_ge(gates_back[4], 32 * (h + 1))
                    dve.wait_ge(f["up"], 2 * u + 1)
                    v.tensor_tensor(hid[:, side, 1, :], hid[:, side, 1, :], gbc[h][:, e, :], ALU.mult
                                    ).then_inc(f["up"], 1)

            def expert1_output(u):
                f, h = ex[1], u // C1
                if u % C1 == C1 - 1:
                    dve.wait_ge(f["y_p"], u + 1)
                    v.tensor_copy(accT[:, half(h)], M_BANK[h][:]).then_inc(f["acc"], 1)

            def finish(h):
                dve.wait_ge(fin_t, h + 1)
                v.scalar_tensor_tensor(xn[:, seqs(h), :], L_BANK[:].rearrange("p (b d) -> p b d", b=HB),
                                       tanh_g[:, 3:4], x_sb[:, seqs(h), :], ALU.mult, ALU.add).then_inc(fin, 1)

            dve.wait_ge(in_x, 16)
            residual_stats(0, 0)
            def split_ctx(h):
                dve.wait_ge(ctx_hi, h + 1)
                v.tensor_tensor(ctxT_lo[:, half(h)], ctx_f[:, half(h)], ctxT_hi[:, half(h)].bitcast(F32), ALU.subtract
                                ).then_inc(ctx_split, 1)

            split_ctx(0)
            normed(0, 0)
            dve.wait_ge(in_w, 16)
            v.tensor_copy(id_bf[:], id_sb[:]).then_inc(mask_done, 1)
            xnT_lo_copy(0, 0)

            def make_mask(h):
                dve.wait_ge(in_mask, 32)
                v.scalar_tensor_tensor(maskb[:, seqs(h), :], by_seq(mask_u8[:, half(h)]), MASKED,
                                       causal_sb[:].unsqueeze(1).to_broadcast([P, HB, P]), ALU.mult, ALU.min
                                       ).then_inc(mask_done, 1)

            make_mask(0)
            dve.wait_ge(consts, 3)
            dve.wait_ge(in_misc, 80)
            dve.wait_ge(in_f0, 64)
            attention0()
            hooks = {0: lambda: residual_stats(1, 1), 1: lambda: normed(1, 1), 3: lambda: xnT_lo_copy(1, 1),
                     4: lambda: route_best(0, 1), 5: lambda: route_gates(0, 1),
                     E0F - 1: lambda: biases1(0), E0F: lambda: residual_stats(2, 0),
                     E0F + 1: lambda: (normed(2, 0), key_hi1(0)),
                     E0F + 2: lambda: values_all1(0),
                     E0F + 3: lambda: (xnT_lo_copy(2, 0), spread_keys1(0, range(H4))),
                     E0F + 4: lambda: (query_hi1(0), values1(0), biases1(1)),
                     E0F + 5: lambda: values1(1),
                     E0F + 6: lambda: key_hi1(1),
                     E0F + 7: lambda: (query_hi1(1), biases1(2))}
            for u in range(2 * E0F):
                expert0(u)
                if u in hooks:
                    hooks[u]()
            dve.wait_ge(in_f1, 48)
            dve.wait_ge(consts, 10)
            slots1({(-1, 3): [lambda: spread_keys1(1, (0, 1))], (0, 0): [lambda: spread_keys1(1, (2, 3))],
                    (0, 2): [lambda: residual_sum(2, 1)], (0, 3): [lambda: statistics(2, 1)],
                    (1, 0): [lambda: normed(2, 1)], (1, 2): [lambda: xnT_lo_copy(2, 1)],
                    (4, 2): [lambda: residual_sum(3, 0)], (4, 3): [lambda: statistics(3, 0)],
                    (5, 0): [lambda: normed(3, 0)], (5, 2): [lambda: xnT_lo_copy(3, 0)],
                    (6, 0): [lambda: route_best(1, 0, (0,))], (6, 1): [lambda: route_best(1, 0, (1,))],
                    (6, 3): [lambda: route_gates(1, 0)]})
            hooks = {0: lambda: xnT_lo_copy(3, 1), 1: lambda: route_best(1, 1), 2: lambda: route_gates(1, 1),
                     C1 + 1: lambda: finish(0)}
            residual_stats(3, 1)
            expert1_hidden(0)
            normed(3, 1)
            for u in range(2 * C1):
                if u + 1 < 2 * C1:
                    expert1_hidden(u + 1)
                expert1_output(u)
                if u in hooks:
                    hooks[u]()
            finish(1)

        @block.tensor
        def _(pe):
            mm = nc.tensor.matmul

            def three(out_, w, m):
                mm(out_, w[0], m[0], start=True, stop=False)
                mm(out_, w[0], m[1], start=False, stop=False)
                return mm(out_, w[1], m[0], start=False, stop=True)

            def four_transposes(src):
                for b in range(HB):
                    ins = nc.tensor.transpose(L_BANK[:, P * b:P * (b + 1)], src(b), id_sb[:])
                return ins

            def acc_transposes(done, h):
                four_transposes(lambda b: accT[:, HALF * h + P * b:HALF * h + P * (b + 1)]).then_inc(done, 1)

            def xn_transposes(n, h):
                pe.wait_ge(ln[n]["xn"], HB * (h + 1))
                four_transposes(lambda b: xn[:, HB * h + b, :]).then_inc(ln[n]["xnT_p"], 1)

            def logits(n, h):
                ne = E0 if n == 0 else E1
                pe.wait_ge(ln[2 * n + 1]["xnT"], 2 * (h + 1))
                for b in range(HB):
                    o = HALF * h + P * b
                    ins = mm(L_BANK[:, ne * b:ne * (b + 1)], xnT[:, o:o + P], gw_sb[n][:], start=True, stop=True)
                ins.then_inc(ex[n]["logit_p"], 1)

            def gate_transposes(n, h):
                rows = E0 if n == 0 else E1S
                pe.wait_ge(ex[n]["gate"], (2 if n == 0 else 1) * (h + 1))
                for b in range(HB):
                    ins = nc.tensor.transpose(L_BANK[0:rows, P * b:P * (b + 1)], gate[:, b, 0:rows], id_sb[:])
                ins.then_inc(ex[n]["gateT_p"], 1)

            def key_or_query0(s, h, p, j):
                a = at[0]
                if p == j == 0:
                    if isinstance(s, int) and s % G == 0:
                        pe.wait_ge(ctx_split, h + 1)
                    pe.wait_ge(a["w_split"], 2 * s + 2)
                if p:
                    pe.wait_ge(a["k_ready"], 4 * s + 2) if j == 0 else pe.wait_ge(a["q_ready"], 2 * s + 1)
                elif j == 0 and not (isinstance(s, int) and s < 2):
                    pe.wait_ge(a["acc"], s - 1)
                elif j == 1 and not (isinstance(s, int) and s == 0):
                    pe.wait_ge(a["v_ready"], 4 * s)
                if isinstance(s, int) and s % G == 0 and j == 1 and p == 0:
                    pe.wait_ge(ln[0]["xnT"], h + 1)
                o = P * p + (0 if j else 256)
                three(M_BANK[j][:], (w_hi[:, o:o + P], w_lo[:, o:o + P]),
                      [m[:, half(h)] for m in ((xnT_hi, xnT_lo) if j else (ctxT_hi, ctxT_lo))]
                      ).then_inc(a["proj"], 1)

            def project_values0(s, h, j):
                a = at[0]
                pe.wait_ge(a["k_ready"], 4 * s + 4) if j == 0 else pe.wait_ge(a["q_ready"], 2 * s + 2)
                if j == 0:
                    pe.wait_ge(a["wv_split"], 2 * s + 2)
                for c in range(2):
                    o = HALF * h + P * (2 * j + c)
                    ins = three(M_BANK[j][:, 256 * c:256 * (c + 1)], [m[:, o:o + P] for m in (ctxT_hi, ctxT_lo)],
                                (w_hi[:, 512:768], w_lo[:, 512:768]))
                ins.then_inc(a["proj"], 1)

            def scores0(s, h, t):
                a = at[0]
                if t == 0:
                    pe.wait_ge(a["q_ready"], 2 * s + 2)
                    pe.wait_ge(a["k_ready"], 4 * s + 4)
                if t >= 2:
                    pe.wait_ge(a["exp"], H4 * (HB * s + t - 1))
                if isinstance(s, int) and s % G == 0 and t == 0:
                    pe.wait_ge(mask_done, 2 + h)
                sb_ = S_BANK[t % 2]
                mm(heads(sb_), id_bf[:], maskb[:, HB * h + t, :].unsqueeze(1).to_broadcast([P, H4, P]),
                   start=True, stop=False)
                for p in range(2):
                    ins = mm(sb_[:, 256 * p:256 * (p + 1)], qT[:, p, P * t:P * (t + 1)],
                             kpad[:, p, t, :, :].rearrange("p h k -> p (h k)"), start=False, stop=(p == 1))
                ins.then_inc(a["scores"], 1)

            def scores1(s, t):
                a = at[1]
                if t == 0:
                    pe.wait_ge(a["q_ready"], s + 1)
                    pe.wait_ge(a["k_ready"], H4 * (s + 1))
                if t >= 2 or s:
                    pe.wait_ge(a["exp"], H4 * (HB * s + t - 1))
                mm(S_BANK[t % 2][:], q1s[:, s % 2, P * t:P * (t + 1)],
                   k1pad[:, s % 2, t].rearrange("p h k -> p (h k)"), start=True, stop=True
                   ).then_inc(a["scores"], 1)

            def transposed1(q):
                s, t = divmod(q, HB)
                if t == 2:
                    pe.wait_ge(at[1]["probsT_a"], s + 1)
                else:
                    pe.wait_ge(at[1]["probsT"], (HB - 1) * s + min(t + 1, HB - 1))

            def turn(n, s, t):
                a = at[n]
                pe.wait_ge(a["probs_n"], HB * s + t + 1)
                if n:
                    if t >= 2 or s:
                        transposed1(HB * s + t - 2)
                elif t >= 2:
                    pe.wait_ge(a["probsT"], HB * s + t - 1)
                for hd in range(H4):
                    ins = nc.tensor.transpose(heads(T_BANK[t % 2])[:, hd, :], probs_n[:, t % 2, hd, :], id_sb[:])
                ins.then_inc(a["probsT_p"], 1)

            def values(n, s, t):
                a = at[n]
                if t == 0:
                    pe.wait_ge(a["v_ready"], 4 * s + 4)
                if n:
                    transposed1(HB * s + t)
                else:
                    pe.wait_ge(a["probsT"], HB * s + t + 1)
                if not (isinstance(s, int) and s == 0 and t == 0):
                    pe.wait_ge(a["oT"], HB * s + t)
                for hd in range(H4):
                    if n == 0:
                        ins = mm(O_BANK[:, P * (hd // 2):P * (hd // 2 + 1)], vpad[:, t, hd, :], probsT[:, t % 2, hd, :],
                                 start=(hd % 2 == 0), stop=(hd % 2 == 1))
                    else:
                        ins = mm(O_BANK[0:GR, 0:P], v1pad[:, s % 2, t, hd, :], probsT[:, t % 2, hd, :],
                                 start=(hd == 0), stop=(hd == H4 - 1))
                ins.then_inc(a["o_p"], 1)

            def output(n, s, bank_read):
                a = at[n]
                pe.wait_ge(a["oT"], HB * (s + 1))
                pe.wait_ge(a["wo_in"], 16 * s + 16)
                pe.wait_ge(*bank_read)
                if n == 0:
                    for p in range(2):
                        ins = mm(M_BANK[0][:], wo_st[:, p, :], oT[:, p, :], start=(p == 0), stop=(p == 1))
                else:
                    ins = mm(M_BANK[0][:], wo1_st[:], oT1[:], start=True, stop=True)
                ins.then_inc(a["y_p"], 1)

            def junction0(s, h, tail, after_turn3=None):
                key_or_query0(s, h, 0, 0)
                if tail:
                    turn(0, s - 1, 2)
                key_or_query0(s, h, 0, 1)
                if tail:
                    values(0, s - 1, 1)
                key_or_query0(s, h, 1, 0)
                if tail:
                    turn(0, s - 1, 3)
                if after_turn3:
                    after_turn3()
                if tail:
                    values(0, s - 1, 2)
                key_or_query0(s, h, 1, 1)
                if tail:
                    values(0, s - 1, 3)

            def keys1(r):
                a = at[1]
                pe.wait_ge(a["w_split"], r + 1)
                if r == 0:
                    pe.wait_ge(at[0]["oT"], 2 * G * HB)
                elif r == 1:
                    pe.wait_ge(a["q_free"], 1)
                elif r == 2:
                    pe.wait_ge(ex[0]["y_g"], 2 * E0F)
                elif r == 3:
                    pe.wait_ge(a["k_free"], 3)
                else:
                    pe.wait_ge(a["acc"], r - 3)
                c = columns1(r).start + P
                three(bank1(r, 0)[:], (w_hi[:, c:c + P], w_lo[:, c:c + P]),
                      [m[:, half(r // G)] for m in (ctxT_hi, ctxT_lo)]).then_inc(a["k_p"], 1)

            def queries1(r):
                a = at[1]
                if r == 0:
                    pe.wait_ge(a["v_sb"], 1)
                elif r == 1:
                    pe.wait_ge(a["k_free"], 2)
                elif r > 2:
                    pe.wait_ge(a["q_free"], r)
                    if r == G + 1:
                        pe.wait_ge(a["v_sb"], 2)
                pe.wait_ge(ln[2]["xnT"], r // G + 1)
                c = columns1(r).start
                three(bank1(r, 1)[:], (w_hi[:, c:c + P], w_lo[:, c:c + P]),
                      [m[:, half(r // G)] for m in (xnT_hi, xnT_lo)]).then_inc(a["q_p"], 1)

            def values_all1(h):
                a = at[1]
                if h == 0:
                    pe.wait_ge(in_w1, 32)
                    pe.wait_ge(a["k_free"], 1)
                else:
                    pe.wait_ge(a["q_free"], G + 1)
                for b in range(HB):
                    o = HALF * h + P * b
                    ins = mm((M_BANK[1] if h else O_BANK)[:, P * b:P * (b + 1)], ctx_f[:, o:o + P], wv1_sb[:],
                             start=True, stop=True)
                ins.then_inc(a["v_p"], 1)

            def slots1(hooks):
                for q in range(-2, TILES1 + 1):
                    s, t = divmod(q, HB)
                    if q + 2 < TILES1:
                        scores1((q + 2) // HB, (q + 2) % HB)
                    if 0 <= q < TILES1:
                        turn(1, s, t)
                    if 0 <= q < TILES1:
                        if t == 2 and s == G - 2:
                            values_all1(1)
                        if t == 1 and s:
                            output(1, s - 1, (at[1]["k_free"], s + 3) if s + 2 < 2 * G else
                                   (at[1]["acc"], s - 1))
                    if q >= 1:
                        values(1, (q - 1) // HB, (q - 1) % HB)
                    if q >= 0 and t == 0 and s + 2 < 2 * G:
                        queries1(s + 2)
                    if q >= -1 and t == 3 and s + 3 < 2 * G:
                        keys1(s + 3)
                    for hook in hooks.get((s, t), ()):
                        hook()
                output(1, 2 * G - 1, (at[1]["acc"], 2 * G - 1))

            def main0(s, h, add, after_v=None, after_scores3=None, end=None):
                a = at[0]
                scores0(s, h, 0)
                project_values0(s, h, 0)
                scores0(s, h, 1)
                project_values0(s, h, 1)
                if after_v:
                    after_v()
                scores0(s, h, 2)
                if add:
                    output(0, s - 1, (a["v_ready"], 4 * s + 2))
                turn(0, s, 0)
                scores0(s, h, 3)
                if after_scores3:
                    after_scores3()
                turn(0, s, 1)
                values(0, s, 0)
                if end:
                    end()

            def attention0():
                junction0(0, 0, False)
                main0(0, 0, False)

                def second_half_in():
                    pe.wait_ge(ln[0]["xnT"], 1)
                    xn_transposes(0, 1)

                junction0(1, 0, True, second_half_in)
                main0(1, 0, True)
                with pe.Fori(2, G) as s:
                    junction0(s, 0, True)
                    main0(s, 0, True)

                def first_half_back():
                    pe.wait_ge(at[0]["acc"], G)
                    pe.wait_ge(ln[0]["xnT"], 2)
                    acc_transposes(ln[1]["accT_t"], 0)

                junction0(G, 1, True)
                main0(G, 1, True, after_scores3=first_half_back)
                junction0(G + 1, 1, True, lambda: xn_transposes(1, 0))
                main0(G + 1, 1, True, after_v=lambda: logits(0, 0))
                junction0(G + 2, 1, True)
                main0(G + 2, 1, True, end=lambda: gate_transposes(0, 0))
                junction0(G + 3, 1, True)
                main0(G + 3, 1, True)
                s = 2 * G - 1
                turn(0, s, 2)
                values(0, s, 1)
                turn(0, s, 3)
                values(0, s, 2)
                values(0, s, 3)
                output(0, s, (at[0]["v_ready"], 4 * s + 4))

            def expert_hidden(n, u):
                f, side, h = ex[n], u % 2, u // (E0F if n == 0 else C1)
                e = u % E0F if n == 0 else pair1(u)
                if u == 0:
                    pe.wait_ge(f["w_hi"], 4)
                    pe.wait_ge(f["w_lo"], 4)
                if u >= 2:
                    if n == 0:
                        pe.wait_ge(f["hid"], 2 * (u - 1))
                    else:
                        pe.wait_ge(f["up"], 2 * (u - 1))
                for c in range(2):
                    o = 2 * P * e + P * c
                    three(bank[2 * side + c][:], (ew_hi[:, o:o + P], ew_lo[:, o:o + P]),
                          [m[:, half(h)] for m in (xnT_hi, xnT_lo)]).then_inc(f["h_p"], 1)

            def expert_output(n, u):
                f, side, e = ex[n], u % 2, u % E0F if n == 0 else pair1(u)
                if u == 0:
                    pe.wait_ge(f["wo_in"], 16)
                if u >= 2 and n == 0:
                    pe.wait_ge(f["y_g"], u - 1)
                elif u == 0:
                    pe.wait_ge(at[n]["acc"], 2 * G)
                if n == 0:
                    pe.wait_ge(f["hid"], 2 * (u + 1))
                    for c in range(C0):
                        ins = mm(M_BANK[side][:], ew2[:, e, c, :], hid[:, side, c, :],
                                 start=(c == 0), stop=(c == C0 - 1))
                else:
                    pe.wait_ge(f["up"], 2 * (u + 1))
                    ins = mm(M_BANK[u // C1][:], ew2[:, e, 0, :], hid[:, side, 1, :],
                             start=(u % C1 == 0), stop=(u % C1 == C1 - 1))
                ins.then_inc(f["y_p"], 1)

            def experts(n, hooks):
                steps = 2 * (E0F if n == 0 else C1)
                expert_hidden(n, 0)
                for u in range(steps):
                    if u in hooks:
                        hooks[u]()
                    if u + 1 < steps:
                        expert_hidden(n, u + 1)
                    expert_output(n, u)

            def sums_back(m, h, complete, bank_read):
                pe.wait_ge(*complete)
                pe.wait_ge(*bank_read)
                acc_transposes(ln[m]["accT_t"] if m < 4 else fin_t, h)

            pe.wait_ge(in_w, 16)
            xn_transposes(0, 0)
            attention0()
            experts(0, {
                0: lambda: sums_back(1, 1, (at[0]["acc"], 2 * G), (ex[0]["gateT"], 1)),
                3: lambda: xn_transposes(1, 1),
                5: lambda: logits(0, 1),
                7: lambda: gate_transposes(0, 1),
                E0F: lambda: keys1(0),
                E0F + 1: lambda: sums_back(2, 0, (ex[0]["acc"], added(E0F - 1)), (ex[0]["gateT"], 2)),
                E0F + 2: lambda: values_all1(0),
                E0F + 3: lambda: xn_transposes(2, 0), E0F + 4: lambda: queries1(0),
                E0F + 6: lambda: keys1(1), E0F + 7: lambda: queries1(1)})
            slots1({(0, 1): [lambda: sums_back(2, 1, (ex[0]["acc"], added(2 * E0F - 1)), (ln[2]["xnT"], 1))],
                    (1, 1): [lambda: xn_transposes(2, 1)],
                    (4, 2): [lambda: sums_back(3, 0, (at[1]["acc"], G), (ln[2]["xnT"], 2))],
                    (5, 1): [lambda: xn_transposes(3, 0)], (5, 3): [lambda: logits(1, 0)],
                    (7, 0): [lambda: gate_transposes(1, 0)]})
            sums_back(3, 1, (at[1]["acc"], 2 * G), (ex[1]["gateT"], 1))
            experts(1, {
                1: lambda: xn_transposes(3, 1),
                2: lambda: logits(1, 1),
                4: lambda: gate_transposes(1, 1),
                C1 + 1: lambda: sums_back(4, 0, (ex[1]["acc"], 1), (ex[1]["gateT"], 2))})
            sums_back(4, 1, (ex[1]["acc"], 2), (fin, 1))


def kernel(**inp):
    import numpy as np
    import concourse.bacc as bacc
    from concourse.bass_utils import run_bass_kernel_spmd as run

    a = {k: np.asarray(v) for k, v in inp.items()}
    t = np.ascontiguousarray
    w0 = np.stack([a[f"L0_xattn_W{n}"].reshape(P, G, 256) for n in "qkv"], 2).reshape(P, G, 768).transpose(1, 0, 2)
    f1 = lambda n: (np.concatenate([a[f"L1_ffn_routed_{n}"], a[f"L1_ffn_shared_{n}"]])
                    .reshape(C1, 2, P, F1).transpose(0, 2, 1, 3).reshape(C1, P, P))
    w2 = np.concatenate([a["L1_ffn_routed_w2"], a["L1_ffn_shared_w2"]]).reshape(C1, P, P)
    head_row = ((np.arange(P)[:, None] % GR // DH1 == np.arange(H4)[None, :])
                & (np.arange(P)[:, None] < 3 * GR)).astype(np.float32)
    group = lambda bias: np.tile(bias.reshape(G, GR), (1, 4)).T
    four = lambda w: np.tile(w.reshape(G, GR, P).transpose(0, 2, 1), (1, 1, 4))
    arrays = {
        "x": a["x"], "ctxT": t(a["ctx_1024"].transpose(2, 0, 1).reshape(P, T)),
        "mask": t(a["mask_BxS2_bf0"]).reshape(T),
        "g_x": a["g_xattn"], "g_f": a["g_ffn"],
        "w0": t(w0), "wo0": t(a["L0_xattn_Wo"].reshape(G, 2, P, P).transpose(0, 2, 1, 3).reshape(G, P, 256)),
        "bo0": a["L0_xattn_bo"].reshape(P, 1),
        "gw0": t(a["L0_ffn_gate_w"].T), "gb0": a["L0_ffn_expert_bias"],
        "f0w1": t(a["L0_ffn_w1"].transpose(0, 2, 1)),
        "f0w2": t(a["L0_ffn_w2"].reshape(E0F, P, C0, P).transpose(0, 3, 2, 1).reshape(E0F, P, C0 * P)),
        "wqk1": t(np.concatenate([four(a["L1_xattn_Wq"]), four(a["L1_xattn_Wk"])], 2)),
        "bqk1": t(np.stack([group(a["L1_xattn_bq"]), group(a["L1_xattn_bk"])], 2).transpose(1, 0, 2)),
        "wv1": t(a["L1_xattn_Wv"].T), "bv1": a["L1_xattn_bv"],
        "wo1": t(a["L1_xattn_Wo"].T.reshape(G, GR, P)), "bo1": a["L1_xattn_bo"].reshape(P, 1),
        "gw1": a["L1_ffn_router_w"], "gb1": a["L1_ffn_router_b"],
        "f1w13": t(np.concatenate([f1("w1"), f1("w3")], 2)), "f1w2": w2,
        "ident": np.eye(P, dtype=np.float32),
        "causal": np.where(np.arange(P)[None, :] > np.arange(P)[:, None], MASKED, 0.0).astype(np.float32),
        "head_row": head_row,
        "rev0": np.arange(E0, 0, -1).astype(np.float32), "rev1": np.arange(E1, 0, -1).astype(np.float32),
    }
    nc = bacc.Bacc("TRN2", target_bir_lowering=False, num_devices=1)
    args = {k: nc.dram_tensor(f"in_{k}", v.shape, mybir.dt.from_np(v.dtype), kind="ExternalInput").ap()
            for k, v in arrays.items()}
    out = nc.dram_tensor("out_x", (B, P, P), F32, kind="ExternalOutput").ap()
    build(nc, out=out, **args)
    r = run(nc, [{f"in_{k}": v for k, v in arrays.items()}], core_ids=[0])
    return r.results[0]["out_x"]
```
